# Optimizing a Trainium2 kernel written in Bass

```python
import numpy as np
import jax
import jax.numpy as jnp

def _softmax(x, axis=-1):
    return jax.nn.softmax(x, axis=axis)

def _gelu(x):
    return jax.nn.gelu(x, approximate=True)

def _silu(x):
    return jax.nn.silu(x)

def _sigmoid(x):
    return jax.nn.sigmoid(x)

def _layernorm(x, axis=-1, eps=1e-05):
    m = jnp.mean(x, axis=axis, keepdims=True)
    v = jnp.var(x, axis=axis, keepdims=True)
    return (x - m) / jnp.sqrt(v + eps)

def _scatter_add(tgt, idx, src, axis=0):
    return tgt.at[idx].add(src)

def _segment_sum(src, seg, n):
    return jax.ops.segment_sum(src, seg, n)
kernel_name = 'mk_vit_tower_d1_tok_img1024_r4_403354'

def setup_inputs(seed: int=0):
    np.random.seed(seed)
    _w = jnp.asarray

    def _rec_inputs():
        import jax
        import jax.numpy as jnp
        _rk = jax.random.key(seed)
        x = -0.000356955 + 1 * jax.random.normal(jax.random.fold_in(_rk, 1), (64, 3, 224, 224), jnp.float32)
        return x
    x = _rec_inputs()

    def _L0_tok_setup():
        import jax, jax.numpy as jnp
        import numpy as np
        PATCH = 16
        H = W = 224
        C = 3
        NP_SIDE = H // PATCH
        NUM_PATCHES = NP_SIDE * NP_SIDE
        PATCH_DIM = C * PATCH * PATCH
        EMBED = 256
        key = jax.random.key(seed)
        k1, k2, k3, k4 = jax.random.split(key, 4)
        B = 128
        raw_pixels = jax.random.normal(k1, (B, C, H, W), dtype=jnp.float32)
        bound = 1.0 / np.sqrt(PATCH_DIM)
        W_embed = jax.random.uniform(k2, (PATCH_DIM, EMBED), minval=-bound, maxval=bound, dtype=jnp.float32)
        b_embed = jax.random.uniform(k3, (EMBED,), minval=-bound, maxval=bound, dtype=jnp.float32)
        pos_embed = jax.random.normal(k4, (1, NUM_PATCHES, EMBED), dtype=jnp.float32)
        return {'raw_pixels': raw_pixels, 'W_embed': W_embed, 'b_embed': b_embed, 'pos_embed': pos_embed}
    _L0_tok_all = _L0_tok_setup()
    _L0_tok_in = {k: v for k, v in _L0_tok_all.items() if k in ('W_embed', 'b_embed', 'pos_embed')}
    del _L0_tok_all

    def _L0_attn_setup():
        import jax, jax.numpy as jnp
        import numpy as np
        B, T, D = (2, 512, 256)
        HV, HK = (16, 8)
        DK, DV = (64, 64)
        K_DIM = HK * DK
        V_DIM = HV * DV
        CONV_DIM = 2 * K_DIM + V_DIM
        KS = 4
        EPS = 1e-06

        def _causal_conv_silu(x, w):
            xp = jnp.pad(x, ((0, 0), (KS - 1, 0), (0, 0)))
            y = sum((xp[:, i:i + x.shape[1], :] * w[:, i] for i in range(KS)))
            return jax.nn.silu(y)

        def _l2norm(x):
            return x * jax.lax.rsqrt(jnp.sum(x * x, -1, keepdims=True) + EPS)

        def _forward(hidden_states, W_qkv, W_z, W_b, W_a, dt_bias, A_log, conv_w, norm_w, W_out):
            b_, t_ = hidden_states.shape[:2]
            mixed_qkv = hidden_states @ W_qkv
            z = (hidden_states @ W_z).reshape(b_, t_, HV, DV)
            beta = jax.nn.sigmoid(hidden_states @ W_b)
            g = -jnp.exp(A_log) * jax.nn.softplus(hidden_states @ W_a + dt_bias)
            mixed_qkv = _causal_conv_silu(mixed_qkv, conv_w)
            q, k, v = jnp.split(mixed_qkv, [K_DIM, 2 * K_DIM], axis=-1)
            q = q.reshape(b_, t_, HK, DK)
            k = k.reshape(b_, t_, HK, DK)
            v = v.reshape(b_, t_, HV, DV)
            rep = HV // HK
            q = jnp.repeat(q, rep, axis=2)
            k = jnp.repeat(k, rep, axis=2)
            q = _l2norm(q) * DK ** (-0.5)
            k = _l2norm(k)
            qT = q.transpose(1, 0, 2, 3)
            kT = k.transpose(1, 0, 2, 3)
            vT = v.transpose(1, 0, 2, 3)
            gT = g.transpose(1, 0, 2)
            bT = beta.transpose(1, 0, 2)

            def step(S, xs):
                q_t, k_t, v_t, g_t, b_t = xs
                S = S * jnp.exp(g_t)[..., None, None]
                kv = jnp.einsum('bhk,bhkv->bhv', k_t, S)
                S = S + jnp.einsum('bhk,bhv->bhkv', k_t, (v_t - kv) * b_t[..., None])
                o_t = jnp.einsum('bhk,bhkv->bhv', q_t, S)
                return (S, o_t)
            S0 = jnp.zeros((b_, HV, DK, DV), jnp.float32)
            _, oT = jax.lax.scan(step, S0, (qT, kT, vT, gT, bT))
            o = oT.transpose(1, 0, 2, 3)
            var = jnp.mean(o * o, axis=-1, keepdims=True)
            o = o * jax.lax.rsqrt(var + EPS) * norm_w * jax.nn.silu(z)
            return o.reshape(b_, t_, V_DIM) @ W_out
        key = jax.random.key(seed)
        ks = jax.random.split(key, 9)
        g = lambda k, shape, sc: jax.random.normal(k, shape, jnp.float32) * sc
        return {'hidden_states': g(ks[0], (B, T, D), 1.0), 'W_qkv': g(ks[1], (D, CONV_DIM), 0.02), 'W_z': g(ks[2], (D, V_DIM), 0.02), 'W_b': g(ks[3], (D, HV), 0.02), 'W_a': g(ks[4], (D, HV), 0.02), 'dt_bias': jnp.ones((HV,), jnp.float32), 'A_log': jnp.log(jax.random.uniform(ks[5], (HV,), jnp.float32, 0.001, 16.0)), 'conv_w': g(ks[6], (CONV_DIM, KS), 0.2), 'norm_w': jnp.ones((DV,), jnp.float32), 'W_out': g(ks[7], (V_DIM, D), 0.02)}
    _L0_attn_all = _L0_attn_setup()
    _L0_attn_in = {k: v for k, v in _L0_attn_all.items() if k in ('W_qkv', 'W_z', 'W_b', 'W_a', 'dt_bias', 'A_log', 'conv_w', 'norm_w', 'W_out')}
    del _L0_attn_all

    def _L0_ffn_setup():
        import jax, jax.numpy as jnp
        import numpy as np
        D_MODEL = 256
        EXPERT_DIM = 128
        N_EXPERTS = 8
        TOP_K = 2

        def _sq_relu(h):
            return jnp.square(jax.nn.relu(h))
        key = jax.random.key(seed)
        ks = jax.random.split(key, 6)
        s = 0.02
        x = jax.random.normal(ks[0], (2, 512, D_MODEL), dtype=jnp.float32)
        Ws1 = jax.random.normal(ks[1], (D_MODEL, EXPERT_DIM), dtype=jnp.float32) * s
        Ws2 = jax.random.normal(ks[2], (EXPERT_DIM, D_MODEL), dtype=jnp.float32) * s
        W1 = jax.random.normal(ks[3], (N_EXPERTS, D_MODEL, EXPERT_DIM), dtype=jnp.float32) * s
        W2 = jax.random.normal(ks[4], (N_EXPERTS, EXPERT_DIM, D_MODEL), dtype=jnp.float32) * s
        Wr = jax.random.normal(ks[5], (D_MODEL, N_EXPERTS), dtype=jnp.float32) * s
        return {'x': x, 'Ws1': Ws1, 'Ws2': Ws2, 'W1': W1, 'W2': W2, 'Wr': Wr}
    _L0_ffn_all = _L0_ffn_setup()
    _L0_ffn_in = {k: v for k, v in _L0_ffn_all.items() if k in ('Ws1', 'Ws2', 'W1', 'W2', 'Wr')}
    del _L0_ffn_all
    return {'x': x, 'L0_tok_W_embed': _L0_tok_in['W_embed'], 'L0_tok_b_embed': _L0_tok_in['b_embed'], 'L0_tok_pos_embed': _L0_tok_in['pos_embed'], 'L0_attn_W_qkv': _L0_attn_in['W_qkv'], 'L0_attn_W_z': _L0_attn_in['W_z'], 'L0_attn_W_b': _L0_attn_in['W_b'], 'L0_attn_W_a': _L0_attn_in['W_a'], 'L0_attn_dt_bias': _L0_attn_in['dt_bias'], 'L0_attn_A_log': _L0_attn_in['A_log'], 'L0_attn_conv_w': _L0_attn_in['conv_w'], 'L0_attn_norm_w': _L0_attn_in['norm_w'], 'L0_attn_W_out': _L0_attn_in['W_out'], 'L0_ffn_Ws1': _L0_ffn_in['Ws1'], 'L0_ffn_Ws2': _L0_ffn_in['Ws2'], 'L0_ffn_W1': _L0_ffn_in['W1'], 'L0_ffn_W2': _L0_ffn_in['W2'], 'L0_ffn_Wr': _L0_ffn_in['Wr']}

def reference(x, L0_tok_W_embed, L0_tok_b_embed, L0_tok_pos_embed, L0_attn_W_qkv, L0_attn_W_z, L0_attn_W_b, L0_attn_W_a, L0_attn_dt_bias, L0_attn_A_log, L0_attn_conv_w, L0_attn_norm_w, L0_attn_W_out, L0_ffn_Ws1, L0_ffn_Ws2, L0_ffn_W1, L0_ffn_W2, L0_ffn_Wr):
    import jax
    import jax.numpy as jnp

    def _L0_tok_ref(raw_pixels, W_embed, b_embed, pos_embed):
        import jax, jax.numpy as jnp
        import numpy as np
        PATCH = 16
        H = W = 224
        C = 3
        NP_SIDE = H // PATCH
        NUM_PATCHES = NP_SIDE * NP_SIDE
        PATCH_DIM = C * PATCH * PATCH
        EMBED = 256
        B = raw_pixels.shape[0]
        patches = raw_pixels.reshape(B, C, NP_SIDE, PATCH, NP_SIDE, PATCH)
        patches = patches.transpose(0, 2, 4, 1, 3, 5).reshape(B, NUM_PATCHES, PATCH_DIM)
        x = jnp.einsum('bnd,de->bne', patches, W_embed) + b_embed
        return x + pos_embed

    def _L0_attn_ref(hidden_states, W_qkv, W_z, W_b, W_a, dt_bias, A_log, conv_w, norm_w, W_out):
        import jax, jax.numpy as jnp
        import numpy as np
        B, T, D = (2, 512, 256)
        HV, HK = (16, 8)
        DK, DV = (64, 64)
        K_DIM = HK * DK
        V_DIM = HV * DV
        CONV_DIM = 2 * K_DIM + V_DIM
        KS = 4
        EPS = 1e-06

        def _causal_conv_silu(x, w):
            xp = jnp.pad(x, ((0, 0), (KS - 1, 0), (0, 0)))
            y = sum((xp[:, i:i + x.shape[1], :] * w[:, i] for i in range(KS)))
            return jax.nn.silu(y)

        def _l2norm(x):
            return x * jax.lax.rsqrt(jnp.sum(x * x, -1, keepdims=True) + EPS)

        def _forward(hidden_states, W_qkv, W_z, W_b, W_a, dt_bias, A_log, conv_w, norm_w, W_out):
            b_, t_ = hidden_states.shape[:2]
            mixed_qkv = hidden_states @ W_qkv
            z = (hidden_states @ W_z).reshape(b_, t_, HV, DV)
            beta = jax.nn.sigmoid(hidden_states @ W_b)
            g = -jnp.exp(A_log) * jax.nn.softplus(hidden_states @ W_a + dt_bias)
            mixed_qkv = _causal_conv_silu(mixed_qkv, conv_w)
            q, k, v = jnp.split(mixed_qkv, [K_DIM, 2 * K_DIM], axis=-1)
            q = q.reshape(b_, t_, HK, DK)
            k = k.reshape(b_, t_, HK, DK)
            v = v.reshape(b_, t_, HV, DV)
            rep = HV // HK
            q = jnp.repeat(q, rep, axis=2)
            k = jnp.repeat(k, rep, axis=2)
            q = _l2norm(q) * DK ** (-0.5)
            k = _l2norm(k)
            qT = q.transpose(1, 0, 2, 3)
            kT = k.transpose(1, 0, 2, 3)
            vT = v.transpose(1, 0, 2, 3)
            gT = g.transpose(1, 0, 2)
            bT = beta.transpose(1, 0, 2)

            def step(S, xs):
                q_t, k_t, v_t, g_t, b_t = xs
                S = S * jnp.exp(g_t)[..., None, None]
                kv = jnp.einsum('bhk,bhkv->bhv', k_t, S)
                S = S + jnp.einsum('bhk,bhv->bhkv', k_t, (v_t - kv) * b_t[..., None])
                o_t = jnp.einsum('bhk,bhkv->bhv', q_t, S)
                return (S, o_t)
            S0 = jnp.zeros((b_, HV, DK, DV), jnp.float32)
            _, oT = jax.lax.scan(step, S0, (qT, kT, vT, gT, bT))
            o = oT.transpose(1, 0, 2, 3)
            var = jnp.mean(o * o, axis=-1, keepdims=True)
            o = o * jax.lax.rsqrt(var + EPS) * norm_w * jax.nn.silu(z)
            return o.reshape(b_, t_, V_DIM) @ W_out
        return _forward(hidden_states, W_qkv, W_z, W_b, W_a, dt_bias, A_log, conv_w, norm_w, W_out)

    def _L0_ffn_ref(x, Ws1, Ws2, W1, W2, Wr):
        import jax, jax.numpy as jnp
        import numpy as np
        D_MODEL = 256
        EXPERT_DIM = 128
        N_EXPERTS = 8
        TOP_K = 2

        def _sq_relu(h):
            return jnp.square(jax.nn.relu(h))
        shape = x.shape
        xf = x.reshape(-1, D_MODEL)
        out_shared = _sq_relu(xf @ Ws1) @ Ws2
        logits = xf @ Wr
        top_vals, top_idx = jax.lax.top_k(logits, TOP_K)
        rw = jax.nn.softmax(top_vals.astype(jnp.float32), axis=-1).astype(x.dtype)
        onehot = jax.nn.one_hot(top_idx, N_EXPERTS, dtype=x.dtype)
        prob = jnp.einsum('tk,tke->te', rw, onehot)
        prob = jnp.trunc(prob)
        h = _sq_relu(jnp.einsum('td,edf->tef', xf, W1))
        y = jnp.einsum('tef,efd->ted', h, W2)
        out_routed = jnp.einsum('ted,te->td', y, prob)
        return (out_shared + out_routed).reshape(shape)
    h = _L0_tok_ref(x, L0_tok_W_embed, L0_tok_b_embed, L0_tok_pos_embed)
    h = h + _L0_attn_ref(_layernorm(h, axis=-1), L0_attn_W_qkv, L0_attn_W_z, L0_attn_W_b, L0_attn_W_a, L0_attn_dt_bias, L0_attn_A_log, L0_attn_conv_w, L0_attn_norm_w, L0_attn_W_out)
    h = h + _L0_ffn_ref(_layernorm(h, axis=-1), L0_ffn_Ws1, L0_ffn_Ws2, L0_ffn_W1, L0_ffn_W2, L0_ffn_Wr)
    return h

_drawn_inputs = setup_inputs


def setup_inputs(seed=0):
    import zlib

    import numpy as np

    out = dict(_drawn_inputs(seed))
    spreads = {'L0_attn_dt_bias': (1.0, 0.6), 'L0_attn_norm_w': (1.0, 0.6)}
    factors = {'L0_tok_b_embed': 2.987, 'L0_attn_W_b': 8.0, 'L0_attn_W_a': 64.0, 'L0_attn_A_log': 4.414}
    for name, (base, spread) in spreads.items():
        noise = np.random.default_rng([zlib.crc32(name.encode()), seed]).standard_normal(out[name].shape)
        drawn = base * np.exp(spread * noise) if base else spread * noise
        out[name] = jnp.asarray(drawn.astype(out[name].dtype))
    for name, factor in factors.items():
        out[name] = (out[name] * factor).astype(out[name].dtype)
    return out
```

```python
from contextlib import ExitStack

import numpy as np

import concourse.bass as bass
from concourse import mybir

F32 = mybir.dt.float32
ALU = mybir.AluOpType
ACT = mybir.ActivationFunctionType
AX = mybir.AxisListType

SIDE = 14
T = SIDE * SIDE
NC = 2
C = T // NC
D = 256
KD = D // 128
PD = 3 * 16 * 16
KP = PD // 128
HK, HV, DH = 8, 16, 64
QT = HK * DH // 128
VT = HV * DH // 128
CT = 2 * QT + VT
VD = HV * DH
TAPS = 4
NP = HV // 4
F = 128
NE = 8
EPS_LN, EPS_HEAD = 1e-5, 1e-6
LEVELS = [1, 2, 4, 8, 16, 32, 64]
NL = len(LEVELS)
LOG_TERMS = [1.0 / 17, 1.0 / 15, 1.0 / 13, 1.0 / 11, 1.0 / 9, 1.0 / 7, 1.0 / 5, 1.0 / 3]

GAIN = dict(
    x_loaded=16, h1_stored=16, out_stored=16,
    embedded=1, h_ready=1, stats_ready=2, var_ready=2, lnv_ready=1, rstd_ready=1, normed=2,
    hT_psum=1, hT_ready=1,
    gates_psum=1, gate_b=1, gate_sum=1, gate_in=1, gate_exp=1, g_ready=1, dve_chain=22,
    proj_psum=CT // 2, raw_ready=CT // 2, tap_ready=CT, conv_step=CT * (TAPS - 1), silu_ready=4,
    z_psum=4, z_ready=4,
    squared=2, sums_psum=1, rln_ready=1, rn_ready=1, rqs_ready=1,
    decay_psum=1, gam_ready=1, scales_ready=1,
    kv_psum=6, k_ready=2, rv_ready=4,
    g_spread=2 * NP, decays_psum=2 * NP, decays_ready=2 * NP, pairs_psum=2 * NP,
    l_part=8 * NP, p_part=4 * NP, lt_psum=2 * NP, lt_ready=2 * NP, pt_psum=2 * NP, pt_ready=2 * NP,
    masked=2 * NP * NL, xn_start=2 * NP, xn_zeroth=2 * NP,
    y_psum=2 * NP * (NL - 1), y_ready=2 * NP * (NL - 1),
    xn_psum=2 * NP * (NL - 2), xn_ready=2 * NP * (NL - 2),
    xt_psum=2 * NP * (NL - 1), xt_ready=2 * NP * NL,
    u_psum=2 * NP, u_ready=2 * NP, us_ready=NP, s_psum=NP, s_ready=NP,
    carry_psum=NP, carry_part=4 * NP, r_ready=NP, o_psum=2 * NP, o0_ready=NP, o1_ready=NP,
    osq_ready=2, oss_ready=2, oms_ready=1, oln_ready=1, orn_ready=1, oc_ready=1, zc_ready=2, og_ready=2,
    ogT_psum=4, ogT_ready=4, attn_psum=2, h1_ready=2,
    stats2_ready=2, var2_ready=2, lnv2_ready=1, rstd2_ready=1, normed2=2,
    xfT_psum=1, xfT_ready=1, hid_psum=1, relu_ready=1, hid_ready=1, ffn_psum=2, out_ready=2,
    router_psum=1, logit_ready=1, best_ready=1, top_ready=2, gap_ready=1, gap_exp=1, prob_step=3,
)

GAIN_ROUTED = dict(
    r_loaded=32, r_stored=16, stats3_ready=2, var3_ready=2, lnv3_ready=1, rstd3_ready=1, normed3=2,
    r_xfT_psum=1, r_xfT_ready=1, r_hid_psum=NE, r_relu_ready=NE, r_hid_ready=NE, r_y_psum=2 * NE, r_added=2 * NE,
    r_prob_ready=1,
)
GAIN.update(GAIN_ROUTED)


def masks():
    i = np.arange(C)
    upto = (i[:, None] <= i[None, :]).astype(np.float32)
    above = (i[:, None] > i[None, :]).astype(np.float32)
    level = []
    for s in LEVELS:
        same = (i[:, None] // (2 * s)) == (i[None, :] // (2 * s))
        level.append((same & ((i[:, None] // s) % 2 == 0) & ((i[None, :] // s) % 2 == 1)).astype(np.float32))
    return np.stack([upto, above, np.eye(C, dtype=np.float32)] + level, axis=1).copy()


def half_selector():
    p = np.arange(128)
    return (p[:, None] // DH == np.arange(2)[None, :]).astype(np.float32)


def build(nc, t, NI):
    with ExitStack() as ctx:
        def sb(name, shape, dt=F32):
            return ctx.enter_context(nc.sbuf_tensor(name, shape, dt))

        sem = {n: ctx.enter_context(nc.semaphore(n)) for n in GAIN}
        for n in ("weights", "setup", "act_setup", "dve_setup", "active_summed", "count_psum",
                  "count_ready", "experts"):
            sem[n] = ctx.enter_context(nc.semaphore(n))
        bank = [ctx.enter_context(nc.psum_tensor(f"bank{i}", [128, 512], F32)) for i in range(8)]

        w_embed = sb("w_embed", [128, KP, D])
        w_qkv = sb("w_qkv", [128, KD, CT * 128])
        w_z = sb("w_z", [128, KD, VD])
        w_ba = sb("w_ba", [128, KD, 2 * HV])
        w_out = sb("w_out", [128, VT, D])
        w_s1 = sb("w_s1", [128, KD, F])
        w_s2 = sb("w_s2", [F, D])
        w_r = sb("w_r", [128, KD, NE])
        conv_w = sb("conv_w", [128, CT, TAPS])
        pos_b = sb("pos_b", [C, NC, D])
        b_row = sb("b_row", [C, D])
        dt_row = sb("dt_row", [C, HV])
        neg_a = sb("neg_a", [C, HV])
        norm_w = sb("norm_w", [128, 1])
        mask = sb("mask", [C, 3 + NL, C])
        ident = sb("ident", [128, 128])
        halves = sb("halves", [128, 2])
        eps_ln = sb("eps_ln", [128, 1])
        eps_head = sb("eps_head", [128, 1])
        ones = sb("ones", [128, 1])

        xT = sb("xT", [128, KP, T])
        h = sb("h", [C, NC, D])
        stats = sb("stats", [C, NC, 6])
        mv = sb("mv", [C, NC, 2])
        rstd = sb("rstd", [C, NC])
        lnv = sb("lnv", [C, NC])
        scratch = sb("scratch", [C, 8])
        hn = sb("hn", [C, NC, D])
        hT = sb("hT", [128, KD, T])
        gate_in = sb("gate_in", [C, NC, 2 * HV])
        gate_a = sb("gate_a", [C, NC, HV])
        gate_e = sb("gate_e", [C, NC, 2 * HV])
        small = sb("small", [C, 6, NC, HV])
        beta = sb("beta", [C, NC, HV])
        g = sb("g", [C, NC, HV])
        raw = sb("raw", [128, CT, T + TAPS - 1])
        qkv = sb("qkv", [128, CT, T])
        zs = sb("zs", [C, NC, VD])
        sq = sb("sq", [128, 2 * QT, T])
        rn = sb("rn", [C, NC, 2 * HK])
        rln = sb("rln", [C, NC, 2 * HK])
        rqs = sb("rqs", [C, NC, HK])
        brk = sb("brk", [C, NC, HV])
        b2 = sb("b2", [C, NC, HV])
        gam = sb("gam", [C, 2, NC, HV])
        b2g = sb("b2g", [C, HV])
        ktok = sb("ktok", [C, NC, HK, DH])
        rv = sb("rv", [C, NC, HV, DH])
        gs = sb("gs", [C, NC, 4, C])
        e_ = sb("e_", [C, NC, 4, C])
        l_ = sb("l_", [C, NC, 4, C])
        p_ = sb("p_", [C, NC, 4, C])
        lt = sb("lt", [C, NC, 4, C])
        pt = sb("pt", [C, NC, 4, C])
        bt = sb("bt", [C, NC, 2, 4, C])
        xn = sb("xn", [C, NC, 4, C])
        xt = sb("xt", [C, NC, 4, C])
        y = sb("y", [C, NC, 4, C])
        u = sb("u", [C, NC, 4, DH])
        us = sb("us", [C, 4, DH])
        st = sb("st", [128, 2 * DH])
        tmp = sb("tmp", [C, 4, DH])
        o = sb("o", [C, NC, HV, DH])
        osq = sb("osq", [C, NC, HV, DH])
        oss = sb("oss", [C, NC, HV])
        oc = sb("oc", [C, 3, NC, HV])
        zc = sb("zc", [C, NC, HV, DH])
        og = sb("og", [C, NC, VD])
        ogT = sb("ogT", [128, NC, VT, C])
        h1 = sb("h1", [C, NC, D])
        xf = sb("xf", [C, NC, D])
        xfT = sb("xfT", [128, KD, T])
        relu = sb("relu", [128, T])
        hid = sb("hid", [128, T])
        out_t = sb("out_t", [C, NC, D])
        logit = sb("logit", [C, NC, NE])
        top = sb("top", [C, NC, 8])
        act_on = sb("act_on", [C, 3, NC])
        prob = sb("prob", [C, NI, NC, NE])
        active = sb("active", [C, NC])
        count = sb("count", [1, 2], mybir.dt.int32)
        r_prob = sb("r_prob", [C, NC, NE])
        w_1, w_2 = w_z, w_out

        upto, above, eye = mask[:, 0, :], mask[:, 1, :], mask[:, 2, :]
        loads = [
            (w_embed, t["w_embed"]), (b_row, t["b_embed"].partition_broadcast(C)), (pos_b, t["pos"]),
            (ident, t["ident"]), (w_ba, t["w_ba"]), (w_qkv, t["w_qkv"]),
            (dt_row, t["dt_bias"].partition_broadcast(C)), (neg_a, t["a_log"].partition_broadcast(C)),
            (conv_w, t["conv_w"]), (w_z, t["w_z"]), (mask, t["masks"]), (halves, t["halves"]),
            (norm_w, t["norm_w"]), (w_out, t["w_out"]), (w_s1, t["w_s1"]), (w_s2, t["w_s2"]), (w_r, t["w_r"]),
        ]
        block = ctx.enter_context(nc.Block())

        def over(ap, n, at):
            shape = list(ap.shape)
            return ap.unsqueeze(at).broadcast_to(shape[:at] + [n] + shape[at:])

        def waits(eng, b):
            def on(name, k=None):
                k = GAIN[name] if k is None else k
                assert 0 < k <= GAIN[name], (name, k)
                eng.wait_ge(sem[name], b * GAIN[name] + k)
            return on

        def nth(p, c):
            return 2 * p + c + 1

        def nth_level(p, lv, c, first=0):
            return (2 * (NL - first)) * p + 2 * (lv - first) + c + 1

        @block.sync
        def _(sp):
            sp.dma_start(xT[:], t["x"][0]).then_inc(sem["x_loaded"], 16)
            for dst, src in loads:
                sp.dma_start(dst[:], src).then_inc(sem["weights"], 16)

            def store(b):
                dst = t["out"][bass.ds(b, 1)].rearrange("a (c p) d -> p (a c) d", c=NC)
                sp.wait_ge(sem["out_ready"], b * GAIN["out_ready"] + GAIN["out_ready"])
                sp.dma_start(dst, out_t[:]).then_inc(sem["out_stored"], 16)
                sp.dma_start(t["h1"][bass.ds(b, 1)].rearrange("a p c d -> p (a c) d"), h1[:]
                             ).then_inc(sem["h1_stored"], 16)

            with sp.Fori(0, NI - 1) as b:
                sp.wait_ge(sem["embedded"], b + 1)
                sp.dma_start(xT[:].rearrange("p k n -> p (k n)"),
                             t["x"][bass.ds(b + 1, 1)].rearrange("a p k n -> p (a k n)")
                             ).then_inc(sem["x_loaded"], 16)
                store(b)
            store(NI - 1)
            sp.wait_ge(sem["out_stored"], 16 * (NI + 1))
            sp.wait_ge(sem["h1_stored"], 16 * (NI + 1))

            sp.wait_ge(sem["count_ready"], 1)
            with sp.If(sp.value_load(count[0:1, 0:1]) > 0):
                sp.dma_start(w_1[:], t["w_1"]).then_inc(sem["experts"], 16)
                sp.dma_start(w_2[:], t["w_2"]).then_inc(sem["experts"], 16)
                with sp.Fori(0, NI) as b:
                    sp.wait_ge(sem["r_stored"], b * 16 + 16)
                    sp.dma_start(h1[:], t["h1"][bass.ds(b, 1)].rearrange("a p c d -> p (a c) d")
                                 ).then_inc(sem["r_loaded"], 16)
                    rows_b = t["out"][bass.ds(b, 1)].rearrange("a (c p) d -> p (a c) d", c=NC)
                    sp.dma_start(out_t[:], rows_b).then_inc(sem["r_loaded"], 16)
                    sp.wait_ge(sem["r_added"], b * GAIN["r_added"] + GAIN["r_added"])
                    sp.dma_start(rows_b, out_t[:]).then_inc(sem["r_stored"], 16)
                sp.wait_ge(sem["r_stored"], 16 * (NI + 1))

        @block.tensor
        def _(pe):
            pe.wait_ge(sem["weights"], 16 * len(loads))
            pe.wait_ge(sem["setup"], 1)
            with pe.Fori(0, NI) as b:
                on = waits(pe, b)

                on("x_loaded")
                for c in range(NC):
                    for k in range(KP):
                        mm = pe.matmul(bank[0][0:C, c * D:(c + 1) * D], xT[:, k, c * C:(c + 1) * C],
                                       w_embed[:, k, :], start=(k == 0), stop=(k == KP - 1))
                mm.then_inc(sem["embedded"], 1)

                for c in range(NC):
                    on("normed", c + 1)
                    for k in range(KD):
                        mm = pe.transpose(bank[1][:, k * T + c * C:k * T + (c + 1) * C],
                                          hn[:, c, k * 128:(k + 1) * 128], ident[0:C, 0:C])
                mm.then_inc(sem["hT_psum"], 1)

                on("hT_ready")
                for c in range(NC):
                    for k in range(KD):
                        mm = pe.matmul(bank[7][0:C, c * 2 * HV:(c + 1) * 2 * HV], hT[:, k, c * C:(c + 1) * C],
                                       w_ba[:, k, :], start=(k == 0), stop=(k == KD - 1))
                mm.then_inc(sem["gates_psum"], 1)

                for j in range(CT // 2):
                    if j >= 4:
                        on("tap_ready", 2 * (j - 3))
                    for r in range(2):
                        tile = 2 * j + r
                        for k in range(KD):
                            mm = pe.matmul(bank[2 + j % 4][:, r * T:(r + 1) * T],
                                           w_qkv[:, k, tile * 128:(tile + 1) * 128], hT[:, k, :],
                                           start=(k == 0), stop=(k == KD - 1))
                    mm.then_inc(sem["proj_psum"], 1)

                for j in range(4):
                    on("tap_ready", 2 * (j + 5))
                    c, half = j // 2, j % 2
                    for k in range(KD):
                        mm = pe.matmul(bank[2 + j][0:C, :], hT[:, k, c * C:(c + 1) * C],
                                       w_z[:, k, half * 512:(half + 1) * 512], start=(k == 0), stop=(k == KD - 1))
                    mm.then_inc(sem["z_psum"], 1)

                on("squared")
                for c in range(NC):
                    for q in range(2 * QT):
                        at = 64 + c * 2 * HK + 2 * q
                        mm = pe.matmul(bank[7][0:C, at:at + 2], sq[:, q, c * C:(c + 1) * C], halves[:],
                                       start=True, stop=True)
                mm.then_inc(sem["sums_psum"], 1)

                on("g_ready")
                pe.matmul(bank[6][0:C, 0:NC * HV], upto, g[:], start=True, stop=True)
                mm = pe.matmul(bank[6][0:C, NC * HV:2 * NC * HV], above, g[:], start=True, stop=True)
                mm.then_inc(sem["decay_psum"], 1)

                on("silu_ready", 2)
                for c in range(NC):
                    for q in range(QT):
                        mm = pe.transpose(bank[c][0:C, q * 128:(q + 1) * 128], qkv[:, QT + q, c * C:(c + 1) * C],
                                          ident[:])
                    mm.then_inc(sem["kv_psum"], 1)
                on("silu_ready", 4)
                for j in range(4):
                    on("z_ready", j + 1)
                    c, half = j // 2, j % 2
                    for q in range(4):
                        mm = pe.transpose(bank[2 + j][0:C, q * 128:(q + 1) * 128],
                                          qkv[:, 2 * QT + 4 * half + q, c * C:(c + 1) * C], ident[:])
                    mm.then_inc(sem["kv_psum"], 1)

                for p in range(NP):
                    for c in range(NC):
                        if p == 0:
                            on("k_ready")
                            on("rv_ready")
                            on("scales_ready")
                        on("g_spread", nth(p, c))
                        if p:
                            on(f"o{c}_ready", p)
                        pe.matmul(bank[4 * c + 1][0:C, 0:4 * C], upto, gs[:, c], start=True, stop=True
                                  ).then_inc(sem["decays_psum"], 1)
                        for kk in range(2):
                            rows = slice(kk * DH, (kk + 1) * DH)
                            kT = qkv[rows, QT + p, c * C:(c + 1) * C]
                            qT = qkv[rows, p, c * C:(c + 1) * C]
                            into = bank[4 * c + 3 * kk]
                            pe.matmul(into[0:C, 0:C], kT, kT, start=True, stop=True)
                            mm = pe.matmul(into[0:C, C:2 * C], qT, kT, start=True, stop=True)
                        mm.then_inc(sem["pairs_psum"], 1)
                    for c in range(NC):
                        on("l_part", 4 * nth(p, c))
                        for h_ in range(4):
                            mm = pe.transpose(bank[4 * c + 2][0:C, h_ * C:(h_ + 1) * C], l_[:, c, h_, :], eye)
                        mm.then_inc(sem["lt_psum"], 1)
                        on("p_part", 2 * nth(p, c))
                        for h_ in range(4):
                            mm = pe.transpose(bank[4 * c + 3][0:C, h_ * C:(h_ + 1) * C], p_[:, c, h_, :], eye)
                        mm.then_inc(sem["pt_psum"], 1)
                    for c in range(NC):
                        on("masked", nth_level(p, 0, c))
                        on("lt_ready", nth(p, c))
                        for h_ in range(4):
                            mm = pe.transpose(bank[4 * c + 2][0:C, h_ * C:(h_ + 1) * C], bt[:, c, 0, h_, :], eye)
                        mm.then_inc(sem["xn_start"], 1)
                    for lv in range(1, NL):
                        last = lv == NL - 1
                        for c in range(NC):
                            on("masked", nth_level(p, lv, c))
                            if lv == 1:
                                on("xt_ready", nth_level(p, 0, c))
                                on("xn_zeroth", nth(p, c))
                            else:
                                on("xn_ready", nth_level(p, lv - 1, c, 1) - 2 * p)
                                on("xt_ready", nth_level(p, lv - 1, c))
                            for h_ in range(4):
                                mm = pe.matmul(bank[4 * c + 2][0:C, h_ * C:(h_ + 1) * C], bt[:, c, lv % 2, h_, :],
                                               xn[:, c, h_, :], start=True, stop=True)
                            mm.then_inc(sem["y_psum"], 1)
                        for c in range(NC):
                            on("y_ready", nth_level(p, lv, c, 1))
                            if not last:
                                for h_ in range(4):
                                    mm = pe.matmul(bank[4 * c][0:C, h_ * C:(h_ + 1) * C], xt[:, c, h_, :],
                                                   y[:, c, h_, :], start=True, stop=True)
                                mm.then_inc(sem["xn_psum"], 1)
                            for h_ in range(4):
                                mm = pe.matmul(bank[4 * c + 1][0:C, h_ * C:(h_ + 1) * C], y[:, c, h_, :],
                                               xt[:, c, h_, :], start=True, stop=True)
                            mm.then_inc(sem["xt_psum"], 1)

                    def u_of(c):
                        for h_ in range(4):
                            mm = pe.matmul(bank[4 * c + 2][0:C, h_ * DH:(h_ + 1) * DH], xt[:, c, h_, :],
                                           rv[:, c, 4 * p + h_, :], start=True, stop=True)
                        mm.then_inc(sem["u_psum"], 1)

                    def o_of(c):
                        for h_ in range(4):
                            mm = pe.matmul(bank[4 * c][0:C, h_ * DH:(h_ + 1) * DH], pt[:, c, h_, :],
                                           u[:, c, h_, :], start=True, stop=True)
                        mm.then_inc(sem["o_psum"], 1)

                    on("xt_ready", nth_level(p, NL - 1, 0))
                    u_of(0)
                    on("us_ready", p + 1)
                    on("pt_ready", nth(p, 0))
                    for kk in range(2):
                        mm = pe.matmul(bank[3][kk * DH:(kk + 1) * DH, 0:2 * DH], ktok[:, 0, 2 * p + kk, :],
                                       us[:, 2 * kk:2 * kk + 2, :], start=True, stop=True)
                    mm.then_inc(sem["s_psum"], 1)
                    on("u_ready", nth(p, 0))
                    on("pt_ready", nth(p, 0))
                    o_of(0)
                    on("s_ready", p + 1)
                    on("pt_ready", nth(p, 1))
                    on("xt_ready", nth_level(p, NL - 1, 1))
                    for kk in range(2):
                        rows = slice(kk * DH, (kk + 1) * DH)
                        into = bank[7 - 2 * kk]
                        pe.matmul(into[0:C, 0:2 * DH], qkv[rows, QT + p, C:T], st[rows, :], start=True, stop=True)
                        mm = pe.matmul(into[0:C, 2 * DH:4 * DH], qkv[rows, p, C:T], st[rows, :],
                                       start=True, stop=True)
                    mm.then_inc(sem["carry_psum"], 1)
                    on("r_ready", p + 1)
                    u_of(1)
                    on("u_ready", nth(p, 1))
                    on("pt_ready", nth(p, 1))
                    o_of(1)

                for c in range(NC):
                    on("og_ready", c + 1)
                    for half in range(2):
                        for q in range(4):
                            tile = 4 * half + q
                            mm = pe.transpose(bank[4 * c + half][:, q * C:(q + 1) * C],
                                              og[:, c, tile * 128:(tile + 1) * 128], eye)
                        mm.then_inc(sem["ogT_psum"], 1)
                for c in range(NC):
                    on("ogT_ready", 2 * (c + 1))
                    for q in range(VT):
                        mm = pe.matmul(bank[4 * c + 2][0:C, 0:D], ogT[:, c, q, :], w_out[:, q, :],
                                       start=(q == 0), stop=(q == VT - 1))
                    mm.then_inc(sem["attn_psum"], 1)

                for c in range(NC):
                    on("normed2", c + 1)
                    for k in range(KD):
                        mm = pe.transpose(bank[3][:, k * T + c * C:k * T + (c + 1) * C],
                                          xf[:, c, k * 128:(k + 1) * 128], eye)
                mm.then_inc(sem["xfT_psum"], 1)
                on("xfT_ready")
                for k in range(KD):
                    mm = pe.matmul(bank[4][:, 0:T], w_s1[:, k, :], xfT[:, k, :], start=(k == 0), stop=(k == KD - 1))
                mm.then_inc(sem["hid_psum"], 1)
                for c in range(NC):
                    for k in range(KD):
                        mm = pe.matmul(bank[7][0:C, 192 + c * NE:192 + (c + 1) * NE], xfT[:, k, c * C:(c + 1) * C],
                                       w_r[:, k, :], start=(k == 0), stop=(k == KD - 1))
                mm.then_inc(sem["router_psum"], 1)
                on("hid_ready")
                for c in range(NC):
                    pe.matmul(bank[5 + c][0:C, 0:D], hid[:, c * C:(c + 1) * C], w_s2[:], start=True, stop=True
                              ).then_inc(sem["ffn_psum"], 1)

            pe.wait_ge(sem["active_summed"], 1)
            pe.matmul(bank[0][0:1, 0:NC], ones[0:C, :], active[:], start=True, stop=True
                      ).then_inc(sem["count_psum"], 1)
            pe.wait_ge(sem["count_ready"], 1)
            with pe.If(pe.value_load(count[0:1, 0:1]) > 0):
                pe.wait_ge(sem["experts"], 32)
                with pe.Fori(0, NI) as b:
                    on = waits(pe, b)
                    for c in range(NC):
                        on("normed3", c + 1)
                        for k in range(KD):
                            mm = pe.transpose(bank[0][:, k * T + c * C:k * T + (c + 1) * C],
                                              xf[:, c, k * 128:(k + 1) * 128], eye)
                    mm.then_inc(sem["r_xfT_psum"], 1)
                    on("r_xfT_ready")
                    for e in range(NE):
                        if e:
                            on("r_relu_ready", e)
                        for k in range(KD):
                            mm = pe.matmul(bank[1][:, 0:T], w_1[:, k, e * F:(e + 1) * F], xfT[:, k, :],
                                           start=(k == 0), stop=(k == KD - 1))
                        mm.then_inc(sem["r_hid_psum"], 1)
                        on("r_hid_ready", e + 1)
                        for c in range(NC):
                            if e:
                                on("r_added", 2 * (e - 1) + c + 1)
                            pe.matmul(bank[2 + c][0:C, 0:D], hid[:, c * C:(c + 1) * C], w_2[:, e, :],
                                      start=True, stop=True).then_inc(sem["r_y_psum"], 1)

        @block.scalar
        def _(act):
            act.wait_ge(sem["weights"], 16 * len(loads))
            nc.scalar.activation(neg_a[:], neg_a[:], ACT.Exp).then_inc(sem["act_setup"], 1)
            act.wait_ge(sem["setup"], 1)
            with act.Fori(0, NI) as b:
                on = waits(act, b)

                def copy(out, in_, name):
                    nc.scalar.activation(out, in_, ACT.Copy).then_inc(sem[name], 1)

                on("var_ready")
                nc.scalar.activation(lnv[:], mv[:, :, 1], ACT.Ln, bias=eps_ln[0:C, :]).then_inc(sem["lnv_ready"], 1)
                on("lnv_ready")
                nc.scalar.activation(rstd[:], lnv[:], ACT.Exp, scale=-0.5).then_inc(sem["rstd_ready"], 1)
                on("hT_psum")
                copy(hT[:], bank[1][:, 0:KD * T].rearrange("p (k n) -> p k n", k=KD), "hT_ready")
                on("gate_in")
                nc.scalar.activation(gate_e[:], gate_in[:], ACT.Exp, scale=-1.0).then_inc(sem["gate_exp"], 1)

                for j in range(CT // 2):
                    on("proj_psum", j + 1)
                    src = bank[2 + j % 4][:, 0:2 * T].rearrange("p (r n) -> p r n", r=2)
                    copy(raw[:, 2 * j:2 * j + 2, TAPS - 1:], src, "raw_ready")
                    for r in range(2):
                        nc.scalar.activation(qkv[:, 2 * j + r, :], src[:, r, :], ACT.Copy,
                                             scale=conv_w[:, 2 * j + r, TAPS - 1:TAPS]
                                             ).then_inc(sem["tap_ready"], 1)
                for j in range(4):
                    on("conv_step", 12 * (j + 1))
                    nc.scalar.activation(qkv[:, 4 * j:4 * j + 4, :], qkv[:, 4 * j:4 * j + 4, :], ACT.Silu
                                         ).then_inc(sem["silu_ready"], 1)
                    c, half = j // 2, j % 2
                    on("z_psum", j + 1)
                    nc.scalar.activation(zs[:, c, half * 512:(half + 1) * 512], bank[2 + j][0:C, :], ACT.Silu
                                         ).then_inc(sem["z_ready"], 1)

                on("sums_psum")
                nc.scalar.activation(rln[:], bank[7][0:C, 64:64 + NC * 2 * HK].rearrange("p (c h) -> p c h", c=NC),
                                     ACT.Ln, bias=eps_head[0:C, :]).then_inc(sem["rln_ready"], 1)
                on("rln_ready")
                nc.scalar.activation(rn[:], rln[:], ACT.Exp, scale=-0.5).then_inc(sem["rn_ready"], 1)
                on("decay_psum")
                nc.scalar.activation(gam[:], bank[6][0:C, 0:2 * NC * HV].rearrange(
                    "p (a c h) -> p a c h", a=2, c=NC), ACT.Exp).then_inc(sem["gam_ready"], 1)
                for c in range(NC):
                    on("kv_psum", c + 1)
                    copy(ktok[:, c], bank[c][0:C, :].rearrange("p (h d) -> p h d", h=HK), "k_ready")

                def quad(ap, w):
                    return ap[0:C, 0:4 * w].rearrange("p (h n) -> p h n", h=4)

                for p in range(NP):
                    for c in range(NC):
                        on("decays_psum", nth(p, c))
                        nc.scalar.activation(e_[:, c], quad(bank[4 * c + 1], C), ACT.Exp
                                             ).then_inc(sem["decays_ready"], 1)
                    for c in range(NC):
                        on("lt_psum", nth(p, c))
                        copy(lt[:, c], quad(bank[4 * c + 2], C), "lt_ready")
                    for lv in range(1, NL):
                        for c in range(NC):
                            on("y_psum", nth_level(p, lv, c, 1))
                            copy(y[:, c], quad(bank[4 * c + 2], C), "y_ready")
                    on("u_psum", nth(p, 0))
                    copy(u[:, 0], quad(bank[2], DH), "u_ready")
                    on("s_psum", p + 1)
                    copy(st[:], bank[3][:, 0:2 * DH], "s_ready")
                    on("o_psum", nth(p, 0))
                    copy(o[:, 0, 4 * p:4 * p + 4, :], quad(bank[0], DH), "o0_ready")
                    on("u_psum", nth(p, 1))
                    copy(u[:, 1], quad(bank[6], DH), "u_ready")

                for c in range(NC):
                    if c == 0:
                        on("o0_ready")
                    else:
                        on("o1_ready")
                    nc.scalar.activation(osq[:, c], o[:, c], ACT.Square).then_inc(sem["osq_ready"], 1)
                on("oms_ready")
                nc.scalar.activation(oc[:, 1], oc[:, 0], ACT.Ln, bias=eps_head[0:C, :], scale=1.0 / DH
                                     ).then_inc(sem["oln_ready"], 1)
                on("oln_ready")
                nc.scalar.activation(oc[:, 2], oc[:, 1], ACT.Exp, scale=-0.5).then_inc(sem["orn_ready"], 1)
                for c in range(NC):
                    for half in range(2):
                        on("ogT_psum", 2 * c + half + 1)
                        copy(ogT[:, c, 4 * half:4 * half + 4, :],
                             bank[4 * c + half][:, 0:4 * C].rearrange("p (q n) -> p q n", q=4), "ogT_ready")
                on("var2_ready")
                nc.scalar.activation(lnv[:], mv[:, :, 1], ACT.Ln, bias=eps_ln[0:C, :]).then_inc(sem["lnv2_ready"], 1)
                on("lnv2_ready")
                nc.scalar.activation(rstd[:], lnv[:], ACT.Exp, scale=-0.5).then_inc(sem["rstd2_ready"], 1)
                on("xfT_psum")
                copy(xfT[:], bank[3][:, 0:KD * T].rearrange("p (k n) -> p k n", k=KD), "xfT_ready")
                on("hid_psum")
                nc.scalar.activation(relu[:], bank[4][:, 0:T], ACT.Relu).then_inc(sem["relu_ready"], 1)
                on("relu_ready")
                nc.scalar.activation(hid[:], relu[:], ACT.Square).then_inc(sem["hid_ready"], 1)
                on("gap_ready")
                nc.scalar.activation(act_on[:, 1], act_on[:, 0], ACT.Exp).then_inc(sem["gap_exp"], 1)

            act.wait_ge(sem["count_ready"], 1)
            with act.If(act.value_load(count[0:1, 0:1]) > 0):
                with act.Fori(0, NI) as b:
                    on = waits(act, b)
                    on("var3_ready")
                    nc.scalar.activation(lnv[:], mv[:, :, 1], ACT.Ln, bias=eps_ln[0:C, :]
                                         ).then_inc(sem["lnv3_ready"], 1)
                    on("lnv3_ready")
                    nc.scalar.activation(rstd[:], lnv[:], ACT.Exp, scale=-0.5).then_inc(sem["rstd3_ready"], 1)
                    on("r_xfT_psum")
                    nc.scalar.activation(xfT[:], bank[0][:, 0:KD * T].rearrange("p (k n) -> p k n", k=KD), ACT.Copy
                                         ).then_inc(sem["r_xfT_ready"], 1)
                    for e in range(NE):
                        on("r_hid_psum", e + 1)
                        nc.scalar.activation(relu[:], bank[1][:, 0:T], ACT.Relu).then_inc(sem["r_relu_ready"], 1)
                        on("r_relu_ready", e + 1)
                        if e:
                            on("r_y_psum", 2 * e)
                        nc.scalar.activation(hid[:], relu[:], ACT.Square).then_inc(sem["r_hid_ready"], 1)

        @block.gpsimd
        def _(pool):
            pool.wait_ge(sem["weights"], 16 * len(loads))
            pool.wait_ge(sem["setup"], 1)
            with pool.Fori(0, NI) as b:
                on = waits(pool, b)

                def times(out, a, c, name):
                    nc.gpsimd.tensor_tensor(out, a, c, ALU.mult).then_inc(sem[name], 1)

                for j in range(2):
                    on("silu_ready", j + 1)
                    times(sq[:, 4 * j:4 * j + 4, :], qkv[:, 4 * j:4 * j + 4, :], qkv[:, 4 * j:4 * j + 4, :], "squared")
                for p in range(NP):
                    for c in range(NC):
                        if p == 0 and c == 0:
                            on("g_ready")
                        if p:
                            on("decays_psum", nth(p - 1, c))
                        times(gs[:, c], over(above, 4, 1), over(g[:, c, 4 * p:4 * p + 4], C, 2), "g_spread")
                    for lv in range(NL):
                        for c in range(NC):
                            if lv == 0:
                                on("lt_ready", nth(p, c))
                            elif lv == 2:
                                on("xn_zeroth", nth(p, c))
                                on("xt_ready", nth_level(p, 0, c))
                            elif lv > 2:
                                on("y_psum", nth_level(p, lv - 2, c, 1))
                            times(bt[:, c, lv % 2], lt[:, c], over(mask[:, 3 + lv, :], 4, 1), "masked")
                for c in range(NC):
                    on("oc_ready")
                    times(zc[:, c], zs[:, c].rearrange("p (h d) -> p h d", h=HV), over(oc[:, 0, c, :], DH, 2),
                          "zc_ready")

        @block.vector
        def _(dve):
            V = nc.vector
            V.memset(raw[:, :, 0:TAPS - 1], 0.0)
            V.memset(eps_ln[:], EPS_LN)
            V.memset(eps_head[:], EPS_HEAD)
            V.memset(ones[:], 1.0)
            V.memset(active[:], 0.0)
            dve.wait_ge(sem["weights"], 16 * len(loads))
            dve.wait_ge(sem["act_setup"], 1)
            V.tensor_tensor(pos_b[:], pos_b[:], over(b_row[:], NC, 1), ALU.add).then_inc(sem["dve_setup"], 1)
            V.tensor_scalar(neg_a[:], neg_a[:], -1.0, None, ALU.mult).then_inc(sem["dve_setup"], 1)
            V.tensor_scalar(w_out[:], w_out[:], norm_w[:], None, ALU.mult).then_inc(sem["dve_setup"], 1)
            dve.wait_ge(sem["dve_setup"], 3)
            V.memset(scratch[:, 0:1], 0.0).then_inc(sem["setup"], 1)
            V.memset(scratch[:, 1:2], 0.0).then_inc(sem["h1_stored"], 16)
            V.memset(scratch[:, 7:8], 0.0).then_inc(sem["r_stored"], 16)
            V.memset(scratch[:, 2:3], 0.0).then_inc(sem["out_stored"], 16)
            def layer_norm(src, dst, tag, on):
                for c in range(NC):
                    V.bn_stats(stats[:, c, :], src[:, c, :]).then_inc(sem[f"stats{tag}_ready"], 1)
                on(f"stats{tag}_ready")
                V.memset(scratch[:, 3:4], 0.0)
                for c in range(NC):
                    V.bn_aggr(mv[:, c, :], stats[:, c, :]).then_inc(sem[f"var{tag}_ready"], 1)
                on(f"rstd{tag}_ready")
                for c in range(NC):
                    V.tensor_scalar(dst[:, c, :], src[:, c, :], mv[:, c, 0:1], rstd[:, c:c + 1],
                                    ALU.subtract, ALU.mult).then_inc(sem[f"normed{tag}"], 1)

            with dve.Fori(0, NI) as b:
                on = waits(dve, b)

                def tt(out, a, c, op, name):
                    V.tensor_tensor(out, a, c, op).then_inc(sem[name], 1)

                on("embedded")
                tt(h[:], bank[0][0:C, :].rearrange("p (c d) -> p c d", c=NC), pos_b[:], ALU.add, "h_ready")
                on("h_ready")
                layer_norm(h, hn, "", on)

                on("gates_psum")
                ba = bank[7][0:C, 0:NC * 2 * HV].rearrange("p (c h) -> p c h", c=NC)
                V.tensor_copy(gate_in[:, :, 0:HV], ba[:, :, 0:HV]).then_inc(sem["gate_b"], 1)
                tt(gate_a[:], ba[:, :, HV:], over(dt_row[:], NC, 1), ALU.add, "gate_sum")
                on("gate_sum")
                V.scalar_tensor_tensor(gate_in[:, :, HV:], gate_a[:], -1.0, gate_a[:], ALU.mult, ALU.max
                                       ).then_inc(sem["gate_in"], 1)
                on("gate_exp")
                chain = [0]

                def link(ins):
                    chain[0] += 1
                    ins.then_inc(sem["dve_chain"], 1)
                    dve.wait_ge(sem["dve_chain"], b * GAIN["dve_chain"] + chain[0])

                e_a = gate_e[:, :, HV:]
                link(V.tensor_scalar(gate_in[:], gate_e[:], 1.0, None, ALU.add))
                link(V.reciprocal(beta[:], gate_in[:, :, 0:HV]))
                link(V.tensor_scalar(small[:, 0], e_a, 2.0, None, ALU.add))
                link(V.reciprocal(small[:, 1], small[:, 0]))
                link(V.tensor_tensor(small[:, 2], small[:, 1], e_a, ALU.mult))
                link(V.tensor_tensor(small[:, 3], small[:, 2], small[:, 2], ALU.mult))
                link(V.tensor_scalar(small[:, 4], small[:, 3], LOG_TERMS[0], None, ALU.mult))
                for term in LOG_TERMS[1:]:
                    link(V.scalar_tensor_tensor(small[:, 4], small[:, 4], term, small[:, 3], ALU.add, ALU.mult))
                link(V.scalar_tensor_tensor(small[:, 4], small[:, 4], 1.0, small[:, 2], ALU.add, ALU.mult))
                link(V.tensor_scalar(small[:, 5], gate_a[:], 0.0, None, ALU.max))
                link(V.scalar_tensor_tensor(small[:, 4], small[:, 4], 2.0, small[:, 5], ALU.mult, ALU.add))
                tt(g[:], small[:, 4], over(neg_a[:], NC, 1), ALU.mult, "g_ready")

                for q in range(4):
                    for i in range(TAPS - 1):
                        for r in range(4):
                            tile = 4 * q + r
                            if i == 0:
                                on("tap_ready", tile + 1)
                            else:
                                on("conv_step", 12 * q + 4 * (i - 1) + r + 1)
                            V.scalar_tensor_tensor(qkv[:, tile, :], raw[:, tile, i:i + T], conv_w[:, tile, i:i + 1],
                                                   qkv[:, tile, :], ALU.mult, ALU.add
                                                   ).then_inc(sem["conv_step"], 1)

                on("rn_ready")
                V.tensor_scalar(rqs[:], rn[:, :, 0:HK], DH ** -0.5, None, ALU.mult).then_inc(sem["rqs_ready"], 1)
                rk = [over(rn[:, c, HK:], 2, 2) for c in range(NC)]
                for c in range(NC):
                    link(V.tensor_tensor(brk[:, c].rearrange("p (k r) -> p k r", r=2),
                                         beta[:, c].rearrange("p (k r) -> p k r", r=2), rk[c], ALU.mult))
                    link(V.tensor_tensor(b2[:, c].rearrange("p (k r) -> p k r", r=2),
                                         brk[:, c].rearrange("p (k r) -> p k r", r=2), rk[c], ALU.mult))
                on("gam_ready")
                tt(b2g[:], b2[:, 1], gam[:, 0, 1], ALU.mult, "scales_ready")
                for j in range(4):
                    on("kv_psum", 3 + j)
                    c, half = j // 2, j % 2
                    tt(rv[:, c, 8 * half:8 * half + 8, :], bank[2 + j][0:C, :].rearrange("p (h d) -> p h d", h=8),
                       over(brk[:, c, 8 * half:8 * half + 8], DH, 2), ALU.mult, "rv_ready")

                def quad(ap, w):
                    return ap[0:C, 0:4 * w].rearrange("p (h n) -> p h n", h=4)

                for p in range(NP):
                    for c in range(NC):
                        on("pairs_psum", nth(p, c))
                        on("decays_ready", nth(p, c))
                        for h_ in range(4):
                            V.scalar_tensor_tensor(l_[:, c, h_, :], bank[4 * c + 3 * (h_ // 2)][0:C, 0:C],
                                                   b2[:, c, 4 * p + h_:4 * p + h_ + 1], e_[:, c, h_, :],
                                                   ALU.mult, ALU.mult).then_inc(sem["l_part"], 1)
                        for kk in range(2):
                            tt(p_[:, c, 2 * kk:2 * kk + 2, :], over(bank[4 * c + 3 * kk][0:C, C:2 * C], 2, 1),
                               e_[:, c, 2 * kk:2 * kk + 2, :], ALU.mult, "p_part")
                    for c in range(NC):
                        on("pt_psum", nth(p, c))
                        tt(pt[:, c], quad(bank[4 * c + 3], C), over(upto, 4, 1), ALU.mult, "pt_ready")
                    for c in range(NC):
                        on("masked", nth_level(p, 0, c))
                        tt(xt[:, c], over(eye, 4, 1), bt[:, c, 0], ALU.subtract, "xt_ready")
                        on("xn_start", nth(p, c))
                        tt(xn[:, c], over(eye, 4, 1), quad(bank[4 * c + 2], C), ALU.subtract, "xn_zeroth")
                    for lv in range(1, NL):
                        for c in range(NC):
                            if lv < NL - 1:
                                on("xn_psum", nth_level(p, lv, c, 1) - 2 * p)
                                tt(xn[:, c], xn[:, c], quad(bank[4 * c], C), ALU.subtract, "xn_ready")
                            on("xt_psum", nth_level(p, lv, c, 1))
                            tt(xt[:, c], xt[:, c], quad(bank[4 * c + 1], C), ALU.subtract, "xt_ready")
                    on("u_ready", nth(p, 0))
                    tt(us[:], u[:, 0], over(gam[:, 1, 0, 4 * p:4 * p + 4], DH, 2), ALU.mult, "us_ready")
                    on("carry_psum", p + 1)
                    for kk in range(2):
                        hs = slice(4 * p + 2 * kk, 4 * p + 2 * kk + 2)
                        src = bank[7 - 2 * kk][0:C, 0:4 * DH].rearrange("p (a r d) -> p a r d", a=2, r=2)
                        tt(tmp[:, 2 * kk:2 * kk + 2, :], src[:, 0], over(b2g[:, hs], DH, 2), ALU.mult, "carry_part")
                        tt(o[:, 1, hs, :], src[:, 1], over(gam[:, 0, 1, hs], DH, 2), ALU.mult, "carry_part")
                    on("carry_part", 4 * (p + 1))
                    tt(rv[:, 1, 4 * p:4 * p + 4, :], rv[:, 1, 4 * p:4 * p + 4, :], tmp[:], ALU.subtract, "r_ready")
                    on("o_psum", nth(p, 1))
                    tt(o[:, 1, 4 * p:4 * p + 4, :], o[:, 1, 4 * p:4 * p + 4, :], quad(bank[4], DH), ALU.add,
                       "o1_ready")

                rq = over(rqs[:].rearrange("p c k -> p (c k)"), 2, 2)

                def by_head(ap):
                    return ap.rearrange("p c (k r) -> p (c k) r", r=2)

                for c in range(NC):
                    on("osq_ready", c + 1)
                    V.tensor_reduce(oss[:, c], osq[:, c], AX.X, ALU.add).then_inc(sem["oss_ready"], 1)
                on("oss_ready")
                link(V.tensor_tensor(by_head(oss[:]), by_head(oss[:]), rq, ALU.mult))
                tt(by_head(oc[:, 0]), by_head(oss[:]), rq, ALU.mult, "oms_ready")
                on("orn_ready")
                tt(by_head(oc[:, 0]), by_head(oc[:, 2]), rq, ALU.mult, "oc_ready")
                for c in range(NC):
                    on("zc_ready", c + 1)
                    tt(og[:, c], o[:, c].rearrange("p h d -> p (h d)"), zc[:, c].rearrange("p h d -> p (h d)"),
                       ALU.mult, "og_ready")
                for c in range(NC):
                    on("attn_psum", c + 1)
                    if c == 0:
                        on("h1_stored")
                    tt(h1[:, c], h[:, c], bank[4 * c + 2][0:C, 0:D], ALU.add, "h1_ready")
                on("h1_ready")
                layer_norm(h1, xf, "2", on)
                on("router_psum")
                lg = bank[7][0:C, 192:192 + NC * NE].rearrange("p (c e) -> p c e", c=NC)
                V.tensor_copy(logit[:], lg).then_inc(sem["logit_ready"], 1)
                for c in range(NC):
                    V.max(top[:, c], lg[:, c]).then_inc(sem["top_ready"], 1)
                on("top_ready")
                tt(act_on[:, 0], top[:, :, 1], top[:, :, 0], ALU.subtract, "gap_ready")
                tt(logit[:], logit[:], over(top[:, :, 0], NE, 2), ALU.is_equal, "best_ready")
                on("best_ready")
                on("gap_exp")
                V.tensor_scalar(act_on[:, 2], act_on[:, 1], 1.0, 1.0, ALU.add, ALU.is_equal
                                ).then_inc(sem["prob_step"], 1)
                on("prob_step", 1)
                tt(active[:], active[:], act_on[:, 2], ALU.add, "prob_step")
                prob_b = prob[:, bass.ds(b, 1)].rearrange("p a c e -> p (a c) e")
                tt(prob_b, logit[:], over(act_on[:, 2], NE, 2), ALU.mult, "prob_step")
                on("out_stored")
                for c in range(NC):
                    on("ffn_psum", c + 1)
                    tt(out_t[:, c], h1[:, c], bank[5 + c][0:C, 0:D], ALU.add, "out_ready")
                assert chain[0] == GAIN["dve_chain"], chain

            on = waits(dve, NI - 1)
            on("prob_step")
            V.memset(scratch[:, 5:6], 0.0).then_inc(sem["active_summed"], 1)
            dve.wait_ge(sem["count_psum"], 1)
            V.tensor_reduce(scratch[0:1, 6:7], bank[0][0:1, 0:NC], AX.X, ALU.add).then_inc(sem["dve_setup"], 1)
            dve.wait_ge(sem["dve_setup"], 4)
            V.tensor_copy(count[0:1, 0:1], scratch[0:1, 6:7]).then_inc(sem["count_ready"], 1)
            dve.wait_ge(sem["count_ready"], 1)
            with dve.If(dve.value_load(count[0:1, 0:1]) > 0):
                with dve.Fori(0, NI) as b:
                    on = waits(dve, b)
                    on("r_loaded")
                    layer_norm(h1, xf, "3", on)
                    V.tensor_copy(r_prob[:], prob[:, bass.ds(b, 1)].rearrange("p a c e -> p (a c) e")
                                  ).then_inc(sem["r_prob_ready"], 1)
                    on("r_prob_ready")
                    for e in range(NE):
                        for c in range(NC):
                            on("r_y_psum", 2 * e + c + 1)
                            if e:
                                on("r_added", 2 * (e - 1) + c + 1)
                            V.scalar_tensor_tensor(out_t[:, c], bank[2 + c][0:C, 0:D], r_prob[:, c, e:e + 1],
                                                   out_t[:, c], ALU.mult, ALU.add).then_inc(sem["r_added"], 1)


def kernel(**inputs):
    import concourse.bacc as bacc
    from concourse.bass_utils import run_bass_kernel_spmd

    def rows(a, k):
        a = np.asarray(a)
        return np.ascontiguousarray(a.reshape(k, 128, a.shape[1]).transpose(1, 0, 2))

    x = np.asarray(inputs["x"])
    n = x.shape[0]
    patches = x.reshape(n, 3, SIDE, 16, SIDE, 16).transpose(0, 1, 3, 5, 2, 4).reshape(n, KP, 128, T)
    arrays = {
        "x": np.ascontiguousarray(patches.transpose(0, 2, 1, 3)),
        "w_embed": rows(inputs["L0_tok_W_embed"], KP),
        "b_embed": np.asarray(inputs["L0_tok_b_embed"]),
        "pos": np.ascontiguousarray(np.asarray(inputs["L0_tok_pos_embed"]).reshape(NC, C, D).transpose(1, 0, 2)),
        "w_qkv": rows(inputs["L0_attn_W_qkv"], KD),
        "w_z": rows(inputs["L0_attn_W_z"], KD),
        "w_ba": rows(np.concatenate([np.asarray(inputs["L0_attn_W_b"]), np.asarray(inputs["L0_attn_W_a"])], 1), KD),
        "dt_bias": np.asarray(inputs["L0_attn_dt_bias"]),
        "a_log": np.asarray(inputs["L0_attn_A_log"]),
        "conv_w": rows(inputs["L0_attn_conv_w"], CT),
        "norm_w": np.ascontiguousarray(np.tile(np.asarray(inputs["L0_attn_norm_w"]), 2)[:, None]),
        "w_out": rows(inputs["L0_attn_W_out"], VT),
        "w_s1": rows(inputs["L0_ffn_Ws1"], KD),
        "w_s2": np.asarray(inputs["L0_ffn_Ws2"]),
        "w_1": np.ascontiguousarray(np.asarray(inputs["L0_ffn_W1"]).reshape(NE, KD, 128, F).transpose(2, 1, 0, 3)
                                    .reshape(128, KD, NE * F)),
        "w_2": np.ascontiguousarray(np.asarray(inputs["L0_ffn_W2"]).transpose(1, 0, 2)),
        "w_r": rows(inputs["L0_ffn_Wr"], KD),
        "masks": masks(), "ident": np.eye(128, dtype=np.float32), "halves": half_selector(),
    }
    nc = bacc.Bacc("TRN2", target_bir_lowering=False, num_devices=1)
    t = {k: nc.dram_tensor(f"in_{k}", a.shape, F32, kind="ExternalInput").ap() for k, a in arrays.items()}
    t["out"] = nc.dram_tensor("out", (n, T, D), F32, kind="ExternalOutput").ap()
    t["h1"] = nc.dram_tensor("h1_kept", (n, C, NC, D), F32, kind="Internal").ap()
    build(nc, t, n)
    r = run_bass_kernel_spmd(nc, [{f"in_{k}": a for k, a in arrays.items()}], core_ids=[0])
    return r.results[0]["out"]
```

```python
from contextlib import ExitStack

import numpy as np

import concourse.bass as bass
from concourse import mybir

F32 = mybir.dt.float32
ALU = mybir.AluOpType
ACT = mybir.ActivationFunctionType
AX = mybir.AxisListType

SIDE = 14
T = SIDE * SIDE
NC = 2
C = T // NC
D = 256
KD = D // 128
PD = 3 * 16 * 16
KP = PD // 128
HK, HV, DH = 8, 16, 64
NP = HV // 4
QH = 4
CT = 4
VT = HV * DH // 128
VD = HV * DH
TAPS = 4
F = 128
NE = 8
EPS_LN, EPS_HEAD = 1e-5, 1e-6
BK = 14
NB = C // BK
NA = NC * QH
NAX = NA + 1
LEVELS = [BK, 2 * BK]
NL = len(LEVELS)
SPLIT = 11
TOP = 4 * BK
LOG_TERMS = [1.0 / 17, 1.0 / 15, 1.0 / 13, 1.0 / 11, 1.0 / 9, 1.0 / 7, 1.0 / 5, 1.0 / 3]
UPTO, ABOVE, EYE, LOWER, SAME, LEVEL = range(6)

GAIN = dict(
    x_loaded=16, h1_stored=16, out_stored=16,
    embedded=1, h_ready=1, stats_ready=2, var_ready=2, vare_ready=1, rstd_ready=1, normed=2,
    hT_psum=1, hT_ready=1, gates_psum=1, gate_b=1, gate_sum=1, gate_in=1, gate_exp=1, g_ready=1, gate_step=17,
    qk_psum=NP, v_psum=NP, raw_ready=2 * NP, tap_ready=4 * NP, conv_step=12 * NP, tanh_ready=2 * NP,
    qk_ready=NP, v_ready=NP, z_psum=NP, ztanh_ready=NP, zs_ready=NP,
    squared=NP, sums_psum=NP, sums_ready=NP, gam_ready=NP, sums_eps=NP, rn_ready=NP, scale_step=4 * NP,
    scales_ready=NP, kt_psum=NP, k_ready=NP, vt_psum=NP, rv_ready=2 * NP,
    g_spread=NA * NP, decays_psum=2 * NP, pairs_psum=2 * NP, decays_ready=2 * NP, l_part=8 * NP, p_part=4 * NP,
    lt_psum=2 * NP, lt_ready=2 * NP, pt_psum=2 * NP, pt_ready=2 * NP, l14_ready=2 * NP, lc_ready=2 * NP,
    lanes_loaded=16 * NP, inv_step=(2 * BK - 3) * NP, inv_t_ready=NP, inv_out=16 * NP, inv_back=16 * NP,
    blocks_out=16 * NP, expanded=NB * NP, expanded_t=NP,
    y_psum=4 * NP, y_ready=4 * NP, xn_psum=2 * NP, xn_ready=2 * NP, x_turn_psum=2 * NP, x_turned=2 * NP,
    xt_psum=2 * NP, xt_ready=2 * NP,
    u1_psum=2 * NP, u1_ready=2 * NP, w_psum=2 * NP, w_ready=2 * NP, u2_psum=2 * NP, u_ready=2 * NP,
    us_ready=NP, s_psum=NP, s_ready=NP, carry_psum=NP, carry_part=4 * NP, r_ready=NP,
    o_psum=2 * NP, o0_ready=NP, o1_ready=NP, osq_ready=NP, oss_ready=NP, oms_ready=NP, oeps_ready=NP, orn_ready=NP,
    oc_ready=NP, zc_ready=NP, og_ready=NP, ogT_psum=NP, ogT_ready=NP,
    attn_psum=1, h1_ready=1, h_moved=1, stats2_ready=2, var2_ready=2, vare2_ready=1, rstd2_ready=1, normed2=2,
    xfT_psum=1, xfT_ready=1, hid_psum=1, relu_ready=1, hid_ready=1, ffn_psum=1, out_ready=1,
    router_psum=1, logit_ready=1, best_ready=1, top_ready=2, gap_ready=1, gap_exp=1, prob_step=3,
    r_loaded=32, r_stored=16, stats3_ready=2, var3_ready=2, vare3_ready=1, rstd3_ready=1, normed3=2,
    r_xfT_psum=1, r_xfT_ready=1, r_hid_psum=NE, r_relu_ready=NE, r_hid_ready=NE, r_y_psum=2 * NE,
    r_added=2 * NE, r_prob_ready=1,
)


def masks():
    i = np.arange(C)
    row, col = i[:, None], i[None, :]
    keep = [row <= col, row > col, row == col,
            (row // BK == col // BK) & (row > col),
            row // BK == col // BK]
    for s in LEVELS:
        keep.append((row // (2 * s) == col // (2 * s)) & (row // s % 2 == 1) & (col // s % 2 == 0))
    kept = np.zeros((128, len(keep), C), np.float32)
    kept[:C] = np.stack(keep, axis=1)
    return kept


def consts():
    p = np.arange(128)
    below = (p[:, None] >= TOP)
    halves = (p[:, None] // DH == np.arange(2)[None, :])
    return (np.concatenate([below, halves], axis=1).astype(np.float32),
            np.tile(np.eye(BK, dtype=np.float32).reshape(1, BK, BK), (NB * NAX, 1, 1)))


def shuffled(ap, width, by_lane):
    assert np.gcd(NAX, BK) == 1
    by_row = [[NAX * width, C], [BK * width, NAX], [1, width]]
    lanes = [[BK * width, NB * NAX], [NAX * width, BK], [1, width]]
    return bass.AP(tensor=ap.tensor, offset=0, ap=lanes if by_lane else by_row)


def build(nc, t, NI):
    with ExitStack() as ctx:
        def sb(name, shape, dt=F32):
            return ctx.enter_context(nc.sbuf_tensor(name, shape, dt))

        sem = {n: ctx.enter_context(nc.semaphore(n)) for n in GAIN}
        for n in ("weights", "setup", "act_setup", "dve_setup", "active_summed", "count_psum", "count_ready",
                  "experts"):
            sem[n] = ctx.enter_context(nc.semaphore(n))
        bank = [ctx.enter_context(nc.psum_tensor(f"bank{i}", [128, 512], F32)) for i in range(8)]

        full = {}

        def rows(name, shape):
            full[name] = sb(name, [128] + shape)
            return full[name][0:C]

        w_embed = sb("w_embed", [128, KP, D])
        w_qkv = sb("w_qkv", [128, KD, NP * CT * 128])
        w_z = sb("w_z", [128, KD, VD])
        w_ba = sb("w_ba", [128, KD, 2 * HV])
        w_out = sb("w_out", [128, VT, D])
        w_s1 = sb("w_s1", [128, KD, F])
        w_s2 = sb("w_s2", [F, D])
        w_r = sb("w_r", [128, KD, NE])
        conv_w = sb("conv_w", [128, NP * CT, TAPS])
        pos_b = sb("pos_b", [C, NC, D])
        b_row = sb("b_row", [C, D])
        dt_row = sb("dt_row", [C, HV])
        neg_a = sb("neg_a", [C, HV])
        norm_w = sb("norm_w", [128, 1])
        mask = rows("mask", [LEVEL + NL, C])
        ident = sb("ident", [128, 128])
        small_c = sb("small_c", [128, 3])
        eye_lane = sb("eye_lane", [NB * NAX, BK, BK])
        eps_ln = sb("eps_ln", [C, NC])
        eps_head = sb("eps_head", [C, NC, QH])
        neg_half = sb("neg_half", [C, NC, QH])
        ones = sb("ones", [128, 1])

        xT = sb("xT", [128, KP, T])
        h_new = sb("h_new", [C, NC, D])
        h = sb("h", [C, NC, D])
        stats = sb("stats", [C, NC, 6])
        mv = sb("mv", [C, NC, 2])
        rstd = sb("rstd", [C, NC])
        vare = sb("vare", [C, NC])
        scratch = sb("scratch", [C, 8])
        hn = sb("hn", [C, NC, D])
        hT = sb("hT", [128, KD, T])
        gate_in = sb("gate_in", [C, NC, 2 * HV])
        gate_a = sb("gate_a", [C, NC, HV])
        gate_e = sb("gate_e", [C, NC, 2 * HV])
        gate_s = sb("gate_s", [C, 6, NC, HV])
        beta = sb("beta", [C, NC, HV])
        g = sb("g", [C, NC, HV])
        h1 = sb("h1", [C, NC, D])
        xf = sb("xf", [C, NC, D])
        xfT = sb("xfT", [128, KD, T])
        relu = sb("relu", [128, T])
        hid = sb("hid", [128, T])
        out_t = sb("out_t", [C, NC, D])
        logit = sb("logit", [C, NC, NE])
        top = sb("top", [C, NC, 8])
        act_on = sb("act_on", [C, 3, NC])
        prob = sb("prob", [C, NI, NC, NE])
        active = sb("active", [C, NC])
        count = sb("count", [1, 2], mybir.dt.int32)
        r_prob = sb("r_prob", [C, NC, NE])
        w_1, w_2 = w_z, w_out

        raw = sb("raw", [128, CT, T + TAPS - 1])
        yc = sb("yc", [128, CT, T])
        th = sb("th", [128, CT, T])
        vb = sb("vb", [128, 2, T])
        sq = sb("sq", [128, 2, T])
        zt = sb("zt", [C, NC, QH * DH])
        ss = sb("ss", [C, NC, QH])
        sse = sb("sse", [C, NC, QH])
        rn = sb("rn", [C, NC, QH])
        b2 = sb("b2", [C, NC, QH])
        brk = sb("brk", [C, NC, QH])
        gs = rows("gs", [NC, QH, C])
        e_ = sb("e_", [C, NC, QH, C])
        l_ = sb("l_", [C, QH, C])
        p_ = sb("p_", [C, QH, C])
        l14 = sb("l14", [C, NC, QH, C])
        lc = sb("lc", [C, NAX, BK])
        qk = sb("qk", [128, NP, 2, T])
        zs = sb("zs", [C, NP, NC, QH, DH])
        rqh = sb("rqh", [C, NP, NC, QH])
        rq2 = sb("rq2", [C, NP, NC, QH])
        gam = sb("gam", [C, NP, 2, NC, QH])
        b2g = sb("b2g", [C, NP, QH])
        ktok = rows("ktok", [NP, NC, 2 * DH])
        rv = rows("rv", [NP, NC, QH, DH])
        lt = rows("lt", [NP, NC, QH, C])
        pt = rows("pt", [NP, NC, QH, C])

        lanes = sb("lanes", [NB * NAX, BK, BK])
        inv = sb("inv", [NB * NAX, BK, 2, BK])
        inv_tmp = sb("inv_tmp", [NB * NAX, BK * BK])
        xc = sb("xc", [C, NAX, 2, BK])

        xn = rows("xn", [2, NC, QH, C])
        xt = rows("xt", [2, NC, QH, C])
        y = rows("y", [NC, QH, C])
        u1 = rows("u1", [NC, QH, DH])
        w_ = rows("w_", [NC, QH, DH])
        u = rows("u", [NC, QH, DH])
        us = rows("us", [QH, DH])
        st = sb("st", [128, 2 * DH])
        tmp = sb("tmp", [C, QH, DH])
        o = sb("o", [C, NC, QH, DH])
        osq = sb("osq", [C, NC, QH, DH])
        oss = sb("oss", [C, 4, NC, QH])
        zc = sb("zc", [C, NC, QH, DH])
        ogT = sb("ogT", [128, NP, 2, NC, C])

        upto, above, eye = (mask[:, k, :] for k in (UPTO, ABOVE, EYE))
        below, halves = small_c[0:C, 0:1], small_c[:, 1:3]
        loads = [
            (w_embed, t["w_embed"]), (b_row, t["b_embed"].partition_broadcast(C)), (pos_b, t["pos"]),
            (ident, t["ident"]), (w_ba, t["w_ba"]), (dt_row, t["dt_bias"].partition_broadcast(C)),
            (neg_a, t["a_log"].partition_broadcast(C)), (w_qkv, t["w_qkv"]), (conv_w, t["conv_w"]),
            (w_z, t["w_z"]), (full["mask"], t["masks"]), (small_c, t["small_c"]), (eye_lane, t["eye_lane"]),
            (norm_w, t["norm_w"]), (w_out, t["w_out"]), (w_s1, t["w_s1"]), (w_s2, t["w_s2"]), (w_r, t["w_r"]),
        ]
        block = ctx.enter_context(nc.Block())

        def over(ap, n, at):
            shape = list(ap.shape)
            return ap.unsqueeze(at).broadcast_to(shape[:at] + [n] + shape[at:])

        def quad(ap, w):
            return ap[0:C, 0:QH * w].rearrange("p (h n) -> p h n", h=QH)

        def value(b, name, k=None):
            k = GAIN[name] if k is None else k
            assert 0 < k <= GAIN[name], (name, k)
            return b * GAIN[name] + k

        def before(b, p, name, n):
            return value(b, name, n * p) if p else value(b - 1, name)

        def nth(p, c):
            return 2 * p + c + 1

        def images(eng, prologue, slot, epilogue):
            prologue()
            for p in range(NP):
                slot(0, p, False, NI > 1)
            if NI > 2:
                with eng.Fori(1, NI - 1) as b:
                    for p in range(NP):
                        slot(b, p, True, True)
            if NI > 1:
                for p in range(NP):
                    slot(NI - 1, p, True, False)
            epilogue()

        def front_of(b, p, more):
            return (b + (p + 2) // NP, (p + 2) % NP) if p + 2 < NP or more else None

        def next_of(b, p, more):
            return (b + (p + 1) // NP, (p + 1) % NP) if p + 1 < NP or more else None

        def is_first(b, p):
            return isinstance(b, int) and b == 0 and p == 0

        @block.sync
        def _(sp):
            def load_x(b):
                sp.dma_start(xT[:].rearrange("p k n -> p (k n)"),
                             t["x"][bass.ds(b, 1)].rearrange("a p k n -> p (a k n)")).then_inc(sem["x_loaded"], 16)

            def to_lanes(b, p):
                sp.wait_ge(sem["lc_ready"], value(b, "lc_ready", 2 * (p + 1)))
                sp.dma_start(shuffled(t["blocks"], BK, by_lane=False), lc[:]).then_inc(sem["blocks_out"], 16)
                sp.wait_ge(sem["blocks_out"], value(b, "blocks_out", 16 * (p + 1)))
                sp.dma_start(lanes[:], shuffled(t["blocks"], BK, by_lane=True)).then_inc(sem["lanes_loaded"], 16)

            def from_lanes(b, p):
                sp.wait_ge(sem["inv_t_ready"], value(b, "inv_t_ready", p + 1))
                sp.dma_start(shuffled(t["inverses"], 2 * BK, by_lane=True), inv[:].rearrange("p i r j -> p i (r j)")
                             ).then_inc(sem["inv_out"], 16)
                sp.wait_ge(sem["inv_out"], value(b, "inv_out", 16 * (p + 1)))
                sp.dma_start(xc[:].rearrange("p a r j -> p a (r j)"), shuffled(t["inverses"], 2 * BK, by_lane=False)
                             ).then_inc(sem["inv_back"], 16)

            def store(b):
                sp.wait_ge(sem["out_ready"], value(b, "out_ready"))
                sp.dma_start(t["out"][bass.ds(b, 1)].rearrange("a (c p) d -> p (a c) d", c=NC), out_t[:]
                             ).then_inc(sem["out_stored"], 16)
                sp.dma_start(t["h1"][bass.ds(b, 1)].rearrange("a p c d -> p (a c) d"), h1[:]
                             ).then_inc(sem["h1_stored"], 16)

            def prologue():
                load_x(0)
                for dst, src in loads:
                    sp.dma_start(dst[:], src).then_inc(sem["weights"], 16)
                if NI > 1:
                    sp.wait_ge(sem["embedded"], value(0, "embedded"))
                    load_x(1)
                to_lanes(0, 0)
                from_lanes(0, 0)
                to_lanes(0, 1)

            def slot(b, p, tail, more):
                a, n = front_of(b, p, more), next_of(b, p, more)
                if n:
                    from_lanes(*n)
                if p == 1 and more == 2:
                    sp.wait_ge(sem["embedded"], value(b + 1, "embedded"))
                    load_x(b + 2)
                if a:
                    to_lanes(*a)
                if p == 0 and tail:
                    store(b - 1)

            def epilogue():
                store(NI - 1)

            prologue()
            for p in range(NP):
                slot(0, p, False, (NI > 1) + (NI > 2))
            if NI > 3:
                with sp.Fori(1, NI - 2) as b:
                    for p in range(NP):
                        slot(b, p, True, 2)
            for b in range(max(1, NI - 2), NI):
                for p in range(NP):
                    slot(b, p, True, NI - 1 - b)
            epilogue()
            sp.wait_ge(sem["out_stored"], 16 * (NI + 1))
            sp.wait_ge(sem["h1_stored"], 16 * (NI + 1))

            sp.wait_ge(sem["count_ready"], 1)
            with sp.If(sp.value_load(count[0:1, 0:1]) > 0):
                sp.dma_start(w_1[:], t["w_1"]).then_inc(sem["experts"], 16)
                sp.dma_start(w_2[:], t["w_2"]).then_inc(sem["experts"], 16)
                with sp.Fori(0, NI) as b:
                    sp.wait_ge(sem["r_stored"], b * 16 + 16)
                    sp.dma_start(h1[:], t["h1"][bass.ds(b, 1)].rearrange("a p c d -> p (a c) d")
                                 ).then_inc(sem["r_loaded"], 16)
                    rows_b = t["out"][bass.ds(b, 1)].rearrange("a (c p) d -> p (a c) d", c=NC)
                    sp.dma_start(out_t[:], rows_b).then_inc(sem["r_loaded"], 16)
                    sp.wait_ge(sem["r_added"], b * GAIN["r_added"] + GAIN["r_added"])
                    sp.dma_start(rows_b, out_t[:]).then_inc(sem["r_stored"], 16)
                sp.wait_ge(sem["r_stored"], 16 * (NI + 1))

        @block.tensor
        def _(pe):
            gs, ktok, rv, lt, pt, xn, xt, y, u1, w_, u, us = (
                full[n] for n in ("gs", "ktok", "rv", "lt", "pt", "xn", "xt", "y", "u1", "w_", "u", "us"))
            upto_all = full["mask"][:, UPTO, :]

            def embed(b):
                pe.wait_ge(sem["x_loaded"], value(b, "x_loaded"))
                for c in range(NC):
                    for k in range(KP):
                        mm = pe.matmul(bank[7][0:C, c * D:(c + 1) * D], xT[:, k, c * C:(c + 1) * C],
                                       w_embed[:, k, :], start=(k == 0), stop=(k == KP - 1))
                mm.then_inc(sem["embedded"], 1)

            def turn(b, src, ready, done):
                pe.wait_ge(sem[ready], value(b, ready))
                for c in range(NC):
                    for k in range(KD):
                        mm = pe.transpose(bank[7][:, k * T + c * C:k * T + (c + 1) * C],
                                          src[:, c, k * 128:(k + 1) * 128], eye)
                mm.then_inc(sem[done], 1)

            def gates(b):
                pe.wait_ge(sem["hT_ready"], value(b, "hT_ready"))
                for c in range(NC):
                    for k in range(KD):
                        mm = pe.matmul(bank[7][0:C, c * 2 * HV:(c + 1) * 2 * HV], hT[:, k, c * C:(c + 1) * C],
                                       w_ba[:, k, :], start=(k == 0), stop=(k == KD - 1))
                mm.then_inc(sem["gates_psum"], 1)

            def project(b, p, half):
                if half == 0:
                    pe.wait_ge(sem["hT_ready"], value(b, "hT_ready"))
                    if not is_first(b, p):
                        pe.wait_ge(sem["lt_ready"], before(b, p, "lt_ready", 2))
                elif not is_first(b, p):
                    pe.wait_ge(sem["pt_ready"], before(b, p, "pt_ready", 2))
                for r in range(2):
                    tile = CT * p + 2 * half + r
                    for k in range(KD):
                        mm = pe.matmul(bank[4 + half][:, r * T:(r + 1) * T], w_qkv[:, k, tile * 128:(tile + 1) * 128],
                                       hT[:, k, :], start=(k == 0), stop=(k == KD - 1))
                mm.then_inc(sem["v_psum" if half else "qk_psum"], 1)

            def project_z(b, p, c):
                if c == 0 and not is_first(b, p):
                    pe.wait_ge(sem["rv_ready"], before(b, p, "rv_ready", 2))
                for k in range(KD):
                    mm = pe.matmul(bank[6][0:C, c * QH * DH:(c + 1) * QH * DH], hT[:, k, c * C:(c + 1) * C],
                                   w_z[:, k, p * QH * DH:(p + 1) * QH * DH], start=(k == 0), stop=(k == KD - 1))
                if c == NC - 1:
                    mm.then_inc(sem["z_psum"], 1)

            def sums(b, p):
                pe.wait_ge(sem["tap_ready"], value(b, "tap_ready", 4 * p + 2))
                pe.wait_ge(sem["squared"], value(b, "squared", p + 1))
                pe.wait_ge(sem["g_ready"], value(b, "g_ready"))
                for c in range(NC):
                    for r in range(2):
                        pe.matmul(bank[4][0:C, c * QH + 2 * r:c * QH + 2 * r + 2], sq[:, r, c * C:(c + 1) * C],
                                  halves, start=True, stop=True)
                for r, side in enumerate((upto, above)):
                    at = NA * (1 + r)
                    mm = pe.matmul(bank[4][0:C, at:at + NA].rearrange("p (c h) -> p c h", c=NC), side,
                                   g[:, :, QH * p:QH * p + QH], start=True, stop=True)
                mm.then_inc(sem["sums_psum"], 1)

            def turn_k(b, p):
                pe.wait_ge(sem["qk_ready"], value(b, "qk_ready", p + 1))
                pe.wait_ge(sem["tap_ready"], value(b, "tap_ready", 4 * p + 4))
                for c in range(NC):
                    mm = pe.transpose(bank[5][0:C, c * 128:(c + 1) * 128], qk[:, p, 1, c * C:(c + 1) * C], ident[:])
                mm.then_inc(sem["kt_psum"], 1)

            def turn_v(b, p):
                pe.wait_ge(sem["p_part"], value(b, "p_part", 4 * (p + 1)))
                pe.wait_ge(sem["v_ready"], value(b, "v_ready", p + 1))
                for c in range(NC):
                    for r in range(2):
                        mm = pe.transpose(bank[6][0:C, (2 * c + r) * 128:(2 * c + r + 1) * 128],
                                          vb[:, r, c * C:(c + 1) * C], ident[:])
                mm.then_inc(sem["vt_psum"], 1)

            def decay_sums(b, p, c):
                pe.wait_ge(sem["g_spread"], value(b, "g_spread", QH * nth(p, c)))
                if c == 0:
                    pe.wait_ge(sem["sums_ready"], value(b, "sums_ready", p + 1))
                    pe.wait_ge(sem["gam_ready"], value(b, "gam_ready", p + 1))
                else:
                    pe.wait_ge(sem["lt_ready"], value(b, "lt_ready", nth(p, 0)))
                pe.matmul(bank[4][0:C, 0:QH * C], upto_all, gs[:, c], start=True, stop=True
                          ).then_inc(sem["decays_psum"], 1)

            def pairs(b, p, c):
                if c == 0:
                    pe.wait_ge(sem["k_ready"], value(b, "k_ready", p + 1))
                    pe.wait_ge(sem["zs_ready"], value(b, "zs_ready", p + 1))
                else:
                    pe.wait_ge(sem["pt_ready"], value(b, "pt_ready", nth(p, 0)))
                for kk in range(2):
                    rows = slice(kk * DH, (kk + 1) * DH)
                    qT, kT = (qk[rows, p, r, c * C:(c + 1) * C] for r in range(2))
                    pe.matmul(bank[5 + kk][0:C, 0:C], kT, kT, start=True, stop=True)
                    mm = pe.matmul(bank[5 + kk][0:C, C:2 * C], qT, kT, start=True, stop=True)
                mm.then_inc(sem["pairs_psum"], 1)

            def turn_squares(b, p, c):
                pe.wait_ge(sem["l_part"], value(b, "l_part", QH * nth(p, c)))
                for h_ in range(QH):
                    mm = pe.transpose(bank[4][0:C, h_ * C:(h_ + 1) * C], l_[:, h_, :], eye)
                mm.then_inc(sem["lt_psum"], 1)
                pe.wait_ge(sem["p_part"], value(b, "p_part", 2 * nth(p, c)))
                for h_ in range(QH):
                    mm = pe.transpose(bank[5][0:C, h_ * C:(h_ + 1) * C], p_[:, h_, :], eye)
                mm.then_inc(sem["pt_psum"], 1)

            def four(into, lhsT, rhs, w):
                for h_ in range(QH):
                    mm = pe.matmul(into[0:C, h_ * w:(h_ + 1) * w], lhsT(h_), rhs(h_), start=True, stop=True)
                return mm

            def level_y(b, p, lv, c):
                par = p % 2
                if lv == 0:
                    pe.wait_ge(sem["expanded"], value(b, "expanded", NB * (p + 1)))
                    if c == 1 and not is_first(b, p):
                        pe.wait_ge(sem["o1_ready"], before(b, p, "o1_ready", 1))
                else:
                    pe.wait_ge(sem["xn_ready"], value(b, "xn_ready", nth(p, c)))
                four(bank[2 * c + lv], lambda h_: lt[:, p, c, h_, :], lambda h_: xn[:, par, c, h_, :], C
                     ).then_inc(sem["y_psum"], 1)

            def level_x(b, p, lv, c):
                par = p % 2
                pe.wait_ge(sem["y_ready"], value(b, "y_ready", 4 * p + 2 * lv + c + 1))
                if lv == 0:
                    if c == 0:
                        if not is_first(b, p):
                            pe.wait_ge(sem["o0_ready"], before(b, p, "o0_ready", 1))
                        pe.wait_ge(sem["expanded_t"], value(b, "expanded_t", p + 1))
                    four(bank[2 * c + 1], lambda h_: xt[:, par, c, h_, :], lambda h_: y[:, c, h_, :], C
                         ).then_inc(sem["xn_psum"], 1)
                else:
                    pe.wait_ge(sem["x_turned"], value(b, "x_turned", nth(p, c)))
                    four(bank[2 * c], lambda h_: y[:, c, h_, :], lambda h_: xt[:, par, c, h_, :], C
                         ).then_inc(sem["xt_psum"], 1)

            def turn_x(b, p, c):
                pe.wait_ge(sem["xn_ready"], value(b, "xn_ready", nth(p, c)))
                for h_ in range(QH):
                    mm = pe.transpose(bank[2 * c][0:C, h_ * C:(h_ + 1) * C], xn[0:C, p % 2, c, h_, :], eye)
                mm.then_inc(sem["x_turn_psum"], 1)

            def solve_1(b, p, c):
                pe.wait_ge(sem["xt_ready"], value(b, "xt_ready", nth(p, c)))
                if c:
                    pe.wait_ge(sem["r_ready"], value(b, "r_ready", p + 1))
                four(bank[2 * c + 1], lambda h_: xt[:, p % 2, c, h_, :], lambda h_: rv[:, p, c, h_, :], DH
                     ).then_inc(sem["u1_psum"], 1)

            def solve_2(b, p, c):
                pe.wait_ge(sem["u1_ready"], value(b, "u1_ready", nth(p, c)))
                four(bank[2 * c], lambda h_: lt[0:TOP, p, c, h_, :], lambda h_: u1[0:TOP, c, h_, :], DH
                     ).then_inc(sem["w_psum"], 1)

            def solve_3(b, p, c):
                pe.wait_ge(sem["w_ready"], value(b, "w_ready", nth(p, c)))
                four(bank[2 * c + 1], lambda h_: xt[:, p % 2, c, h_, :], lambda h_: w_[:, c, h_, :], DH
                     ).then_inc(sem["u2_psum"], 1)

            def state(b, p):
                pe.wait_ge(sem["us_ready"], value(b, "us_ready", p + 1))
                for kk in range(2):
                    mm = pe.matmul(bank[0][kk * DH:(kk + 1) * DH, 0:2 * DH], ktok[:, p, 0, kk * DH:(kk + 1) * DH],
                                   us[:, 2 * kk:2 * kk + 2, :], start=True, stop=True)
                mm.then_inc(sem["s_psum"], 1)

            def carry(b, p):
                pe.wait_ge(sem["s_ready"], value(b, "s_ready", p + 1))
                pe.wait_ge(sem["xt_ready"], value(b, "xt_ready", nth(p, 1)))
                for kk in range(2):
                    rows = slice(kk * DH, (kk + 1) * DH)
                    pe.matmul(bank[3 - kk][0:C, 0:2 * DH], qk[rows, p, 1, C:T], st[rows, :], start=True, stop=True)
                    mm = pe.matmul(bank[3 - kk][0:C, 2 * DH:4 * DH], qk[rows, p, 0, C:T], st[rows, :],
                                   start=True, stop=True)
                mm.then_inc(sem["carry_psum"], 1)

            def output(b, p, c):
                pe.wait_ge(sem["u_ready"], value(b, "u_ready", nth(p, c)))
                four(bank[1 + c], lambda h_: pt[:, p, c, h_, :], lambda h_: u[:, c, h_, :], DH
                     ).then_inc(sem["o_psum"], 1)

            def turn_out(b, p, tail, more):
                if p:
                    pe.wait_ge(sem["ogT_ready"], value(b, "ogT_ready", p))
                elif tail:
                    pe.wait_ge(sem["out_ready"], value(b - 1, "out_ready"))
                if p == 1 and more:
                    pe.wait_ge(sem["gate_sum"], value(b + 1, "gate_sum"))
                    pe.wait_ge(sem["gate_b"], value(b + 1, "gate_b"))
                pe.wait_ge(sem["og_ready"], value(b, "og_ready", p + 1))
                for r in range(2):
                    for c in range(NC):
                        at = (2 * r + c) * C
                        mm = pe.transpose(bank[7][:, at:at + C], o[:, c, 2 * r:2 * r + 2, :], eye)
                mm.then_inc(sem["ogT_psum"], 1)

            def attention_out(b):
                pe.wait_ge(sem["ogT_ready"], value(b, "ogT_ready"))
                for c in range(NC):
                    for q in range(VT):
                        mm = pe.matmul(bank[7][0:C, c * D:(c + 1) * D], ogT[:, q // 2, q % 2, c, :], w_out[:, q, :],
                                       start=(q == 0), stop=(q == VT - 1))
                mm.then_inc(sem["attn_psum"], 1)

            def expert_in(b):
                pe.wait_ge(sem["xfT_ready"], value(b, "xfT_ready"))
                for k in range(KD):
                    mm = pe.matmul(bank[7][:, 0:T], w_s1[:, k, :], xfT[:, k, :], start=(k == 0), stop=(k == KD - 1))
                mm.then_inc(sem["hid_psum"], 1)

            def router(b):
                pe.wait_ge(sem["relu_ready"], value(b, "relu_ready"))
                for c in range(NC):
                    for k in range(KD):
                        mm = pe.matmul(bank[7][0:C, c * NE:(c + 1) * NE], xfT[:, k, c * C:(c + 1) * C],
                                       w_r[:, k, :], start=(k == 0), stop=(k == KD - 1))
                mm.then_inc(sem["router_psum"], 1)

            def expert_out(b):
                pe.wait_ge(sem["hid_ready"], value(b, "hid_ready"))
                pe.wait_ge(sem["logit_ready"], value(b, "logit_ready"))
                pe.wait_ge(sem["top_ready"], value(b, "top_ready"))
                for c in range(NC):
                    mm = pe.matmul(bank[7][0:C, c * D:(c + 1) * D], hid[:, c * C:(c + 1) * C], w_s2[:],
                                   start=True, stop=True)
                mm.then_inc(sem["ffn_psum"], 1)

            def front_alone(b, p):
                project(b, p, 0)
                project(b, p, 1)
                project_z(b, p, 0)
                project_z(b, p, 1)
                sums(b, p)
                turn_k(b, p)
                for c in range(NC):
                    decay_sums(b, p, c)
                    pairs(b, p, c)
                    turn_squares(b, p, c)
                turn_v(b, p)

            def prologue():
                pe.wait_ge(sem["weights"], 16 * len(loads))
                pe.wait_ge(sem["setup"], 1)
                embed(0)
                turn(0, hn, "normed", "hT_psum")
                gates(0)
                front_alone(0, 0)
                front_alone(0, 1)

            def slot(b, p, tail, more):
                a = front_of(b, p, more)
                is_tail, is_head = p == 0 and tail, p == 1 and more
                level_y(b, p, 0, 0)
                if a:
                    project(*a, 0)
                level_y(b, p, 0, 1)
                level_x(b, p, 0, 0)
                level_x(b, p, 0, 1)
                if a:
                    project(*a, 1)
                level_y(b, p, 1, 0)
                turn_x(b, p, 0)
                level_y(b, p, 1, 1)
                turn_x(b, p, 1)
                if a:
                    project_z(*a, 0)
                level_x(b, p, 1, 0)
                if a:
                    project_z(*a, 1)
                level_x(b, p, 1, 1)
                if is_head:
                    turn_out(b, p - 1, tail, more)
                if is_tail:
                    turn_out(b - 1, NP - 1, True, True)
                solve_1(b, p, 0)
                if a:
                    sums(*a)
                if is_head:
                    pe.wait_ge(sem["ogT_ready"], value(b, "ogT_ready", 1))
                    embed(b + 1)
                if is_tail:
                    attention_out(b - 1)
                solve_2(b, p, 0)
                if a:
                    turn_k(*a)
                if p and not is_head:
                    turn_out(b, p - 1, tail, more)
                if a and (is_tail or is_head):
                    decay_sums(*a, 0)
                solve_3(b, p, 0)
                if a and not (is_tail or is_head):
                    decay_sums(*a, 0)
                if a:
                    pairs(*a, 0)
                state(b, p)
                output(b, p, 0)
                carry(b, p)
                if a:
                    turn_squares(*a, 0)
                if is_tail:
                    turn(b - 1, xf, "normed2", "xfT_psum")
                if is_head:
                    turn(b + 1, hn, "normed", "hT_psum")
                if a:
                    decay_sums(*a, 1)
                solve_1(b, p, 1)
                if a:
                    pairs(*a, 1)
                solve_2(b, p, 1)
                if is_tail:
                    expert_in(b - 1)
                if is_head:
                    gates(b + 1)
                if a:
                    turn_squares(*a, 1)
                solve_3(b, p, 1)
                if a:
                    turn_v(*a)
                if is_tail:
                    router(b - 1)
                output(b, p, 1)
                if is_tail:
                    expert_out(b - 1)

            def epilogue():
                b = NI - 1
                turn_out(b, NP - 1, True, False)
                attention_out(b)
                turn(b, xf, "normed2", "xfT_psum")
                expert_in(b)
                router(b)
                expert_out(b)

            images(pe, prologue, slot, epilogue)

            pe.wait_ge(sem["active_summed"], 1)
            pe.matmul(bank[0][0:1, 0:NC], ones[0:C, :], active[:], start=True, stop=True
                      ).then_inc(sem["count_psum"], 1)
            pe.wait_ge(sem["count_ready"], 1)
            with pe.If(pe.value_load(count[0:1, 0:1]) > 0):
                pe.wait_ge(sem["experts"], 32)
                with pe.Fori(0, NI) as b:
                    for c in range(NC):
                        pe.wait_ge(sem["normed3"], value(b, "normed3", c + 1))
                        for k in range(KD):
                            mm = pe.transpose(bank[0][:, k * T + c * C:k * T + (c + 1) * C],
                                              xf[:, c, k * 128:(k + 1) * 128], eye)
                    mm.then_inc(sem["r_xfT_psum"], 1)
                    pe.wait_ge(sem["r_xfT_ready"], value(b, "r_xfT_ready"))
                    for e in range(NE):
                        if e:
                            pe.wait_ge(sem["r_relu_ready"], value(b, "r_relu_ready", e))
                        for k in range(KD):
                            mm = pe.matmul(bank[1][:, 0:T], w_1[:, k, e * F:(e + 1) * F], xfT[:, k, :],
                                           start=(k == 0), stop=(k == KD - 1))
                        mm.then_inc(sem["r_hid_psum"], 1)
                        pe.wait_ge(sem["r_hid_ready"], value(b, "r_hid_ready", e + 1))
                        for c in range(NC):
                            if e:
                                pe.wait_ge(sem["r_added"], value(b, "r_added", 2 * (e - 1) + c + 1))
                            pe.matmul(bank[2 + c][0:C, 0:D], hid[:, c * C:(c + 1) * C], w_2[:, e, :],
                                      start=True, stop=True).then_inc(sem["r_y_psum"], 1)

        @block.scalar
        def _(act):
            def evacuate(b, p, half):
                if not is_first(b, p):
                    used = "v_ready" if half else "qk_ready"
                    act.wait_ge(sem[used], before(b, p, used, 1))
                act.wait_ge(sem["v_psum" if half else "qk_psum"], value(b, "v_psum" if half else "qk_psum", p + 1))
                src = bank[4 + half][:, 0:2 * T].rearrange("p (r n) -> p r n", r=2)
                nc.scalar.activation(raw[:, 2 * half:2 * half + 2, TAPS - 1:], src, ACT.Copy
                                     ).then_inc(sem["raw_ready"], 1)
                for r in range(2):
                    tile = CT * p + 2 * half + r
                    nc.scalar.activation(yc[:, 2 * half + r, :], src[:, r, :], ACT.Copy,
                                         scale=conv_w[:, tile, TAPS - 1:TAPS]).then_inc(sem["tap_ready"], 1)

            def spread(b, p, c):
                act.wait_ge(sem["g_ready"], value(b, "g_ready"))
                if c == 0 and not is_first(b, p):
                    act.wait_ge(sem["decays_psum"], before(b, p, "decays_psum", 2))
                for h_ in range(QH):
                    nc.scalar.activation(gs[:, c, h_, :], above, ACT.Copy, scale=g[:, c, QH * p + h_:QH * p + h_ + 1]
                                         ).then_inc(sem["g_spread"], 1)

            def tanh_conv(b, p, half):
                act.wait_ge(sem["conv_step"], value(b, "conv_step", 12 * p + 6 * (half + 1)))
                nc.scalar.activation(th[:, 2 * half:2 * half + 2, :], yc[:, 2 * half:2 * half + 2, :], ACT.Tanh
                                     ).then_inc(sem["tanh_ready"], 1)

            def square_qk(b, p):
                act.wait_ge(sem["qk_ready"], value(b, "qk_ready", p + 1))
                nc.scalar.activation(sq[:], qk[:, p], ACT.Square).then_inc(sem["squared"], 1)

            def tanh_z(b, p):
                if not is_first(b, p):
                    act.wait_ge(sem["zs_ready"], before(b, p, "zs_ready", 1))
                act.wait_ge(sem["z_psum"], value(b, "z_psum", p + 1))
                nc.scalar.activation(zt[:], bank[6][0:C, :].rearrange("p (c n) -> p c n", c=NC), ACT.Tanh, scale=0.5
                                     ).then_inc(sem["ztanh_ready"], 1)

            def read_sums(b, p):
                if not is_first(b, p):
                    act.wait_ge(sem["rn_ready"], before(b, p, "rn_ready", 1))
                act.wait_ge(sem["sums_psum"], value(b, "sums_psum", p + 1))
                nc.scalar.activation(ss[:], bank[4][0:C, 0:NA].rearrange("p (c h) -> p c h", c=NC), ACT.Copy
                                     ).then_inc(sem["sums_ready"], 1)
                nc.scalar.activation(gam[:, p], bank[4][0:C, NA:3 * NA].rearrange("p (r c h) -> p r c h", r=2, c=NC),
                                     ACT.Exp).then_inc(sem["gam_ready"], 1)

            def read_k(b, p):
                act.wait_ge(sem["kt_psum"], value(b, "kt_psum", p + 1))
                nc.scalar.activation(ktok[:, p], bank[5][0:C, 0:2 * 128].rearrange("p (c n) -> p c n", c=NC), ACT.Copy
                                     ).then_inc(sem["k_ready"], 1)

            def decays(b, p, c):
                if c == 0 and not is_first(b, p):
                    act.wait_ge(sem["p_part"], before(b, p, "p_part", 4))
                act.wait_ge(sem["decays_psum"], value(b, "decays_psum", nth(p, c)))
                nc.scalar.activation(e_[:, c], quad(bank[4], C), ACT.Exp).then_inc(sem["decays_ready"], 1)

            def read_lt(b, p, c):
                act.wait_ge(sem["lt_psum"], value(b, "lt_psum", nth(p, c)))
                nc.scalar.activation(lt[:, p, c], quad(bank[4], C), ACT.Copy).then_inc(sem["lt_ready"], 1)

            def turn_inverse(b, p):
                if not is_first(b, p):
                    act.wait_ge(sem["inv_out"], before(b, p, "inv_out", 16))
                    act.wait_ge(sem["expanded"], before(b, p, "expanded", NB))
                    act.wait_ge(sem["expanded_t"], before(b, p, "expanded_t", 1))
                act.wait_ge(sem["inv_step"], value(b, "inv_step", (2 * BK - 3) * (p + 1)))
                nc.scalar.activation(inv[:, :, 1], inv[:, :, 0].rearrange("p i j -> p j i"), ACT.Copy
                                     ).then_inc(sem["inv_t_ready"], 1)

            def expand(b, p):
                act.wait_ge(sem["inv_back"], value(b, "inv_back", 16 * (p + 1)))
                for q in range(NB):
                    nc.scalar.activation(xn[:, p % 2].rearrange("p c h (q j) -> p (c h) q j", q=NB)[:, :, q, :],
                                         xc[:, 0:NA, 0], ACT.Copy, scale=mask[:, SAME, q * BK:q * BK + 1]
                                         ).then_inc(sem["expanded"], 1)

            def read_xt(b, p, c):
                act.wait_ge(sem["x_turn_psum"], value(b, "x_turn_psum", nth(p, c)))
                nc.scalar.activation(xt[:, p % 2, c], quad(bank[2 * c], C), ACT.Copy).then_inc(sem["x_turned"], 1)

            def read_u1(b, p, c):
                act.wait_ge(sem["u1_psum"], value(b, "u1_psum", nth(p, c)))
                nc.scalar.activation(u1[:, c], quad(bank[2 * c + 1], DH), ACT.Copy).then_inc(sem["u1_ready"], 1)

            def read_w(b, p, c):
                act.wait_ge(sem["w_psum"], value(b, "w_psum", nth(p, c)))
                nc.scalar.activation(w_[:, c], quad(bank[2 * c], DH), ACT.Copy, scale=below
                                     ).then_inc(sem["w_ready"], 1)

            def read_state(b, p):
                act.wait_ge(sem["s_psum"], value(b, "s_psum", p + 1))
                nc.scalar.activation(st[:], bank[0][:, 0:2 * DH], ACT.Copy).then_inc(sem["s_ready"], 1)

            def read_o0(b, p):
                if not is_first(b, p):
                    act.wait_ge(sem["ogT_psum"], before(b, p, "ogT_psum", 1))
                act.wait_ge(sem["o_psum"], value(b, "o_psum", nth(p, 0)))
                nc.scalar.activation(o[:, 0], quad(bank[1], DH), ACT.Copy).then_inc(sem["o0_ready"], 1)

            def square_o(b, p):
                act.wait_ge(sem["o0_ready"], value(b, "o0_ready", p + 1))
                act.wait_ge(sem["o1_ready"], value(b, "o1_ready", p + 1))
                nc.scalar.activation(osq[:], o[:], ACT.Square).then_inc(sem["osq_ready"], 1)

            def read_ogT(b, p):
                act.wait_ge(sem["ogT_psum"], value(b, "ogT_psum", p + 1))
                nc.scalar.activation(ogT[:, p],
                                     bank[7][:, 0:2 * NC * C].rearrange("p (r c n) -> p r c n", r=2, c=NC), ACT.Copy
                                     ).then_inc(sem["ogT_ready"], 1)

            def read_turned(b, dst, psum, ready):
                act.wait_ge(sem[psum], value(b, psum))
                nc.scalar.activation(dst[:], bank[7][:, 0:KD * T].rearrange("p (k n) -> p k n", k=KD), ACT.Copy
                                     ).then_inc(sem[ready], 1)

            def gate_exps(b):
                act.wait_ge(sem["gate_b"], value(b, "gate_b"))
                act.wait_ge(sem["gate_in"], value(b, "gate_in"))
                nc.scalar.activation(gate_e[:], gate_in[:], ACT.Exp, scale=-1.0).then_inc(sem["gate_exp"], 1)

            def squared_relu(b):
                act.wait_ge(sem["hid_psum"], value(b, "hid_psum"))
                nc.scalar.activation(relu[:], bank[7][:, 0:T], ACT.Relu).then_inc(sem["relu_ready"], 1)
                act.wait_ge(sem["relu_ready"], value(b, "relu_ready"))
                nc.scalar.activation(hid[:], relu[:], ACT.Square).then_inc(sem["hid_ready"], 1)

            def gap_exp(b):
                act.wait_ge(sem["gap_ready"], value(b, "gap_ready"))
                nc.scalar.activation(act_on[:, 1], act_on[:, 0], ACT.Exp).then_inc(sem["gap_exp"], 1)

            def front_alone(b, p):
                for half in range(2):
                    spread(b, p, half)
                    evacuate(b, p, half)
                tanh_conv(b, p, 0)
                tanh_z(b, p)
                square_qk(b, p)
                tanh_conv(b, p, 1)
                read_sums(b, p)
                read_k(b, p)
                for c in range(NC):
                    decays(b, p, c)
                    read_lt(b, p, c)

            def prologue():
                act.wait_ge(sem["weights"], 16 * len(loads))
                nc.scalar.activation(neg_a[:], neg_a[:], ACT.Exp).then_inc(sem["act_setup"], 1)
                act.wait_ge(sem["setup"], 1)
                read_turned(0, hT, "hT_psum", "hT_ready")
                gate_exps(0)
                front_alone(0, 0)
                turn_inverse(0, 0)
                expand(0, 0)
                front_alone(0, 1)

            def slot(b, p, tail, more):
                a, n = front_of(b, p, more), next_of(b, p, more)
                is_tail, is_head = p == 0 and tail, p == 1 and more
                if a:
                    evacuate(*a, 0)
                    spread(*a, 0)
                    evacuate(*a, 1)
                read_xt(b, p, 0)
                read_xt(b, p, 1)
                if a:
                    spread(*a, 1)
                    tanh_conv(*a, 0)
                    tanh_z(*a)
                    square_qk(*a)
                if is_head:
                    read_ogT(b, p - 1)
                if is_tail:
                    read_ogT(b - 1, NP - 1)
                read_u1(b, p, 0)
                if a:
                    read_sums(*a)
                read_w(b, p, 0)
                if a:
                    read_k(*a)
                if p and not is_head:
                    read_ogT(b, p - 1)
                if a:
                    decays(*a, 0)
                if a:
                    tanh_conv(*a, 1)
                read_state(b, p)
                read_o0(b, p)
                if n:
                    turn_inverse(*n)
                if a:
                    read_lt(*a, 0)
                if is_tail:
                    read_turned(b - 1, xfT, "xfT_psum", "xfT_ready")
                if is_head:
                    read_turned(b + 1, hT, "hT_psum", "hT_ready")
                if a:
                    decays(*a, 1)
                read_u1(b, p, 1)
                read_w(b, p, 1)
                if is_tail:
                    squared_relu(b - 1)
                if is_head:
                    gate_exps(b + 1)
                if a:
                    read_lt(*a, 1)
                if n:
                    expand(*n)
                square_o(b, p)
                if is_tail:
                    gap_exp(b - 1)

            def epilogue():
                b = NI - 1
                read_ogT(b, NP - 1)
                read_turned(b, xfT, "xfT_psum", "xfT_ready")
                squared_relu(b)
                gap_exp(b)

            images(act, prologue, slot, epilogue)

            act.wait_ge(sem["count_ready"], 1)
            with act.If(act.value_load(count[0:1, 0:1]) > 0):
                with act.Fori(0, NI) as b:
                    act.wait_ge(sem["r_xfT_psum"], value(b, "r_xfT_psum"))
                    nc.scalar.activation(xfT[:], bank[0][:, 0:KD * T].rearrange("p (k n) -> p k n", k=KD), ACT.Copy
                                         ).then_inc(sem["r_xfT_ready"], 1)
                    for e in range(NE):
                        act.wait_ge(sem["r_hid_psum"], value(b, "r_hid_psum", e + 1))
                        nc.scalar.activation(relu[:], bank[1][:, 0:T], ACT.Relu).then_inc(sem["r_relu_ready"], 1)
                        act.wait_ge(sem["r_relu_ready"], value(b, "r_relu_ready", e + 1))
                        if e:
                            act.wait_ge(sem["r_y_psum"], value(b, "r_y_psum", 2 * e))
                        nc.scalar.activation(hid[:], relu[:], ACT.Square).then_inc(sem["r_hid_ready"], 1)

        @block.gpsimd
        def _(pool):
            def layer_root(b, tag):
                pool.wait_ge(sem[f"var{tag}_ready"], value(b, f"var{tag}_ready"))
                nc.gpsimd.tensor_tensor(vare[:], mv[:, :, 1], eps_ln[:], ALU.add).then_inc(sem[f"vare{tag}_ready"], 1)
                pool.wait_ge(sem[f"vare{tag}_ready"], value(b, f"vare{tag}_ready"))
                nc.gpsimd.tensor_tensor(rstd[:], vare[:], neg_half[:, :, 0], ALU.pow
                                        ).then_inc(sem[f"rstd{tag}_ready"], 1)

            def norms(b, p):
                pool.wait_ge(sem["sums_ready"], value(b, "sums_ready", p + 1))
                nc.gpsimd.tensor_tensor(sse[:], ss[:], eps_head[:], ALU.add).then_inc(sem["sums_eps"], 1)
                pool.wait_ge(sem["sums_eps"], value(b, "sums_eps", p + 1))
                if not is_first(b, p):
                    pool.wait_ge(sem["scales_ready"], before(b, p, "scales_ready", 1))
                nc.gpsimd.tensor_tensor(rn[:], sse[:], neg_half[:], ALU.pow).then_inc(sem["rn_ready"], 1)

            def blocks_of(b, p, c):
                if not is_first(b, p):
                    pool.wait_ge(sem["lc_ready"], before(b, p, "lc_ready", 2))
                pool.wait_ge(sem["l_part"], value(b, "l_part", QH * nth(p, c)))
                nc.gpsimd.tensor_tensor(l14[:, c], l_[:], over(mask[:, LOWER, :], QH, 1), ALU.mult
                                        ).then_inc(sem["l14_ready"], 1)

            def invert(b, p, part):
                per = 2 * BK - 3
                x = inv[:, :, 0]
                if part == 0:
                    pool.wait_ge(sem["lanes_loaded"], value(b, "lanes_loaded", 16 * (p + 1)))
                    if not is_first(b, p):
                        pool.wait_ge(sem["inv_out"], before(b, p, "inv_out", 16))
                    nc.gpsimd.tensor_tensor(x, eye_lane[:], lanes[:], ALU.subtract).then_inc(sem["inv_step"], 1)
                for j in range(1, SPLIT) if part == 0 else range(SPLIT, BK - 1):
                    n = BK - 1 - j
                    taken = inv_tmp[:, 0:n * j].rearrange("p (i m) -> p i m", i=n)
                    pool.wait_ge(sem["inv_step"], value(b, "inv_step", per * p + 2 * j - 1))
                    nc.gpsimd.tensor_tensor(taken, over(lanes[:, j + 1:, j], j, 2), over(x[:, j, 0:j], n, 1), ALU.mult
                                            ).then_inc(sem["inv_step"], 1)
                    pool.wait_ge(sem["inv_step"], value(b, "inv_step", per * p + 2 * j))
                    nc.gpsimd.tensor_tensor(x[:, j + 1:, 0:j], x[:, j + 1:, 0:j], taken, ALU.subtract
                                            ).then_inc(sem["inv_step"], 1)

            def expand_t(b, p):
                pool.wait_ge(sem["inv_back"], value(b, "inv_back", 16 * (p + 1)))
                nc.gpsimd.tensor_tensor(xt[:, p % 2].rearrange("p c h (q j) -> p (c h) q j", q=NB),
                                        over(xc[:, 0:NA, 1], NB, 2),
                                        over(mask[:, SAME, :].rearrange("p (q j) -> p q j", q=NB), NA, 1), ALU.mult
                                        ).then_inc(sem["expanded_t"], 1)

            def head_norm(b, p):
                pool.wait_ge(sem["oms_ready"], value(b, "oms_ready", p + 1))
                nc.gpsimd.tensor_tensor(oss[:, 2], oss[:, 1], eps_head[:], ALU.add).then_inc(sem["oeps_ready"], 1)
                pool.wait_ge(sem["oeps_ready"], value(b, "oeps_ready", p + 1))
                nc.gpsimd.tensor_tensor(oss[:, 3], oss[:, 2], neg_half[:], ALU.pow).then_inc(sem["orn_ready"], 1)

            def scale_gate(b, p):
                pool.wait_ge(sem["orn_ready"], value(b, "orn_ready", p + 1))
                nc.gpsimd.tensor_tensor(oss[:, 0], oss[:, 3], rqh[:, p], ALU.mult).then_inc(sem["oc_ready"], 1)
                pool.wait_ge(sem["oc_ready"], value(b, "oc_ready", p + 1))
                nc.gpsimd.tensor_tensor(zc[:], zs[:, p], over(oss[:, 0], DH, 3), ALU.mult).then_inc(sem["zc_ready"], 1)

            def front_alone(b, p):
                norms(b, p)
                for c in range(NC):
                    blocks_of(b, p, c)

            def prologue():
                pool.wait_ge(sem["weights"], 16 * len(loads))
                pool.wait_ge(sem["setup"], 1)
                layer_root(0, "")
                front_alone(0, 0)
                invert(0, 0, 0)
                invert(0, 0, 1)
                expand_t(0, 0)
                front_alone(0, 1)

            def slot(b, p, tail, more):
                a, n = front_of(b, p, more), next_of(b, p, more)
                before_ = (b, p - 1) if p else (b - 1, NP - 1) if tail else None
                if before_:
                    head_norm(*before_)
                    scale_gate(*before_)
                if n:
                    invert(*n, 0)
                if a:
                    norms(*a)
                if n:
                    invert(*n, 1)
                if p == 0 and tail:
                    layer_root(b - 1, "2")
                if p == 1 and more:
                    layer_root(b + 1, "")
                if a:
                    blocks_of(*a, 0)
                    blocks_of(*a, 1)
                if n:
                    expand_t(*n)

            def epilogue():
                head_norm(NI - 1, NP - 1)
                scale_gate(NI - 1, NP - 1)
                layer_root(NI - 1, "2")

            images(pool, prologue, slot, epilogue)

            pool.wait_ge(sem["count_ready"], 1)
            with pool.If(pool.value_load(count[0:1, 0:1]) > 0):
                with pool.Fori(0, NI) as b:
                    layer_root(b, "3")

        @block.vector
        def _(dve):
            V = nc.vector

            def layer_stats(b, src, tag):
                for c in range(NC):
                    V.bn_stats(stats[:, c, :], src[:, c, :]).then_inc(sem[f"stats{tag}_ready"], 1)
                dve.wait_ge(sem[f"stats{tag}_ready"], value(b, f"stats{tag}_ready"))
                V.memset(scratch[:, 3:4], 0.0)
                for c in range(NC):
                    V.bn_aggr(mv[:, c, :], stats[:, c, :]).then_inc(sem[f"var{tag}_ready"], 1)

            def layer_scale(b, src, dst, tag):
                dve.wait_ge(sem[f"rstd{tag}_ready"], value(b, f"rstd{tag}_ready"))
                for c in range(NC):
                    V.tensor_scalar(dst[:, c, :], src[:, c, :], mv[:, c, 0:1], rstd[:, c:c + 1],
                                    ALU.subtract, ALU.mult).then_inc(sem[f"normed{tag}"], 1)

            def embedding(b):
                dve.wait_ge(sem["embedded"], value(b, "embedded"))
                V.tensor_tensor(h_new[:], bank[7][0:C, :].rearrange("p (c d) -> p c d", c=NC), pos_b[:], ALU.add
                                ).then_inc(sem["h_ready"], 1)
                dve.wait_ge(sem["h_ready"], value(b, "h_ready"))
                layer_stats(b, h_new, "")

            def gate_inputs(b):
                dve.wait_ge(sem["gates_psum"], value(b, "gates_psum"))
                ba = bank[7][0:C, 0:NC * 2 * HV].rearrange("p (c h) -> p c h", c=NC)
                V.tensor_copy(gate_in[:, :, 0:HV], ba[:, :, 0:HV]).then_inc(sem["gate_b"], 1)
                V.tensor_tensor(gate_a[:], ba[:, :, HV:], over(dt_row[:], NC, 1), ALU.add).then_inc(sem["gate_sum"], 1)
                dve.wait_ge(sem["gate_sum"], value(b, "gate_sum"))
                V.scalar_tensor_tensor(gate_in[:, :, HV:], gate_a[:], -1.0, gate_a[:], ALU.mult, ALU.max
                                       ).then_inc(sem["gate_in"], 1)

            def gate_fractions(b):
                e_a = gate_e[:, :, HV:]
                dve.wait_ge(sem["gate_exp"], value(b, "gate_exp"))
                V.tensor_scalar(gate_in[:], gate_e[:], 1.0, None, ALU.add).then_inc(sem["gate_step"], 1)
                V.tensor_scalar(gate_s[:, 0], e_a, 2.0, None, ALU.add).then_inc(sem["gate_step"], 1)
                dve.wait_ge(sem["gate_step"], value(b, "gate_step", 2))
                V.reciprocal(beta[:], gate_in[:, :, 0:HV]).then_inc(sem["gate_step"], 1)
                V.reciprocal(gate_s[:, 1], gate_s[:, 0]).then_inc(sem["gate_step"], 1)
                dve.wait_ge(sem["gate_step"], value(b, "gate_step", 4))
                V.tensor_tensor(gate_s[:, 2], gate_s[:, 1], e_a, ALU.mult).then_inc(sem["gate_step"], 1)
                dve.wait_ge(sem["gate_step"], value(b, "gate_step", 5))
                V.tensor_tensor(gate_s[:, 3], gate_s[:, 2], gate_s[:, 2], ALU.mult).then_inc(sem["gate_step"], 1)

            def gate_series(b, terms):
                for k in terms:
                    dve.wait_ge(sem["gate_step"], value(b, "gate_step", 6 + k))
                    if k == 0:
                        V.tensor_scalar(gate_s[:, 4], gate_s[:, 3], LOG_TERMS[0], None, ALU.mult
                                        ).then_inc(sem["gate_step"], 1)
                    else:
                        V.scalar_tensor_tensor(gate_s[:, 4], gate_s[:, 4], LOG_TERMS[k], gate_s[:, 3],
                                               ALU.add, ALU.mult).then_inc(sem["gate_step"], 1)

            def gate_logs(b):
                k = 6 + len(LOG_TERMS)
                V.tensor_scalar(gate_s[:, 5], gate_a[:], 0.0, None, ALU.max).then_inc(sem["gate_step"], 1)
                dve.wait_ge(sem["gate_step"], value(b, "gate_step", k + 1))
                V.scalar_tensor_tensor(gate_s[:, 4], gate_s[:, 4], 1.0, gate_s[:, 2], ALU.add, ALU.mult
                                       ).then_inc(sem["gate_step"], 1)
                dve.wait_ge(sem["gate_step"], value(b, "gate_step", k + 2))
                V.scalar_tensor_tensor(gate_s[:, 4], gate_s[:, 4], 2.0, gate_s[:, 5], ALU.mult, ALU.add
                                       ).then_inc(sem["gate_step"], 1)
                dve.wait_ge(sem["gate_step"], value(b, "gate_step", k + 3))
                V.tensor_tensor(g[:], gate_s[:, 4], over(neg_a[:], NC, 1), ALU.mult).then_inc(sem["g_ready"], 1)

            def residual(b):
                dve.wait_ge(sem["attn_psum"], value(b, "attn_psum"))
                dve.wait_ge(sem["h1_stored"], value(b, "h1_stored"))
                V.tensor_tensor(h1[:], h[:], bank[7][0:C, :].rearrange("p (c d) -> p c d", c=NC), ALU.add
                                ).then_inc(sem["h1_ready"], 1)
                dve.wait_ge(sem["h1_ready"], value(b, "h1_ready"))

            def move_h(b):
                V.tensor_copy(h[:], h_new[:]).then_inc(sem["h_moved"], 1)

            def routing(b):
                dve.wait_ge(sem["router_psum"], value(b, "router_psum"))
                lg = bank[7][0:C, 0:NC * NE].rearrange("p (c e) -> p c e", c=NC)
                V.tensor_copy(logit[:], lg).then_inc(sem["logit_ready"], 1)
                for c in range(NC):
                    V.max(top[:, c], lg[:, c]).then_inc(sem["top_ready"], 1)
                dve.wait_ge(sem["top_ready"], value(b, "top_ready"))
                V.tensor_tensor(act_on[:, 0], top[:, :, 1], top[:, :, 0], ALU.subtract).then_inc(sem["gap_ready"], 1)
                dve.wait_ge(sem["logit_ready"], value(b, "logit_ready"))
                V.tensor_tensor(logit[:], logit[:], over(top[:, :, 0], NE, 2), ALU.is_equal
                                ).then_inc(sem["best_ready"], 1)

            def finish(b):
                dve.wait_ge(sem["out_stored"], value(b, "out_stored"))
                dve.wait_ge(sem["ffn_psum"], value(b, "ffn_psum"))
                V.tensor_tensor(out_t[:], h1[:], bank[7][0:C, :].rearrange("p (c d) -> p c d", c=NC), ALU.add
                                ).then_inc(sem["out_ready"], 1)
                dve.wait_ge(sem["gap_exp"], value(b, "gap_exp"))
                V.tensor_scalar(act_on[:, 2], act_on[:, 1], 1.0, 1.0, ALU.add, ALU.is_equal
                                ).then_inc(sem["prob_step"], 1)
                dve.wait_ge(sem["prob_step"], value(b, "prob_step", 1))
                dve.wait_ge(sem["best_ready"], value(b, "best_ready"))
                V.tensor_tensor(active[:], active[:], act_on[:, 2], ALU.add).then_inc(sem["prob_step"], 1)
                prob_b = prob[:, bass.ds(b, 1)].rearrange("p a c e -> p (a c) e")
                V.tensor_tensor(prob_b, logit[:], over(act_on[:, 2], NE, 2), ALU.mult).then_inc(sem["prob_step"], 1)

            def convolve(b, p, half, taps=range(TAPS - 1)):
                if taps[0] == 0:
                    dve.wait_ge(sem["raw_ready"], value(b, "raw_ready", 2 * p + half + 1))
                for i in taps:
                    for r in range(2):
                        tile = 2 * half + r
                        if i == 0:
                            dve.wait_ge(sem["tap_ready"], value(b, "tap_ready", 4 * p + tile + 1))
                        else:
                            done = 12 * p + 6 * half + 2 * (i - 1) + r + 1
                            dve.wait_ge(sem["conv_step"], value(b, "conv_step", done))
                        w = conv_w[:, CT * p + tile, i:i + 1]
                        V.scalar_tensor_tensor(yc[:, tile, :], raw[:, tile, i:i + T], w, yc[:, tile, :],
                                               ALU.mult, ALU.add).then_inc(sem["conv_step"], 1)

            def silu(b, p, half):
                if half and not is_first(b, p):
                    dve.wait_ge(sem["vt_psum"], before(b, p, "vt_psum", 1))
                dve.wait_ge(sem["tanh_ready"], value(b, "tanh_ready", 2 * p + half + 1))
                s = slice(2 * half, 2 * half + 2)
                V.scalar_tensor_tensor(vb[:] if half else qk[:, p], th[:, s, :], 1.0, yc[:, s, :], ALU.add, ALU.mult
                                       ).then_inc(sem["v_ready" if half else "qk_ready"], 1)

            def silu_z(b, p):
                dve.wait_ge(sem["ztanh_ready"], value(b, "ztanh_ready", p + 1))
                V.scalar_tensor_tensor(zs[:, p].rearrange("p c h d -> p c (h d)"), zt[:], 1.0,
                                       bank[6][0:C, :].rearrange("p (c n) -> p c n", c=NC), ALU.add, ALU.mult
                                       ).then_inc(sem["zs_ready"], 1)

            def scales(b, p):
                dve.wait_ge(sem["rn_ready"], value(b, "rn_ready", p + 1))

                def by_key(ap):
                    return ap.rearrange("p c (k r) -> p c k r", r=2)

                rq, rk = over(rn[:, :, 0:2], 2, 3), over(rn[:, :, 2:4], 2, 3)
                V.tensor_tensor(by_key(brk[:]), by_key(beta[:, :, QH * p:QH * p + QH]), rk, ALU.mult
                                ).then_inc(sem["scale_step"], 1)
                V.tensor_scalar(by_key(rqh[:, p]), rq, DH ** -0.5, None, ALU.mult).then_inc(sem["scale_step"], 1)
                dve.wait_ge(sem["scale_step"], value(b, "scale_step", 4 * p + 1))
                V.tensor_tensor(by_key(b2[:]), by_key(brk[:]), rk, ALU.mult).then_inc(sem["scale_step"], 1)
                dve.wait_ge(sem["scale_step"], value(b, "scale_step", 4 * p + 2))
                V.scalar_tensor_tensor(rq2[:, p], rqh[:, p], 1.0 / DH, rqh[:, p], ALU.mult, ALU.mult
                                       ).then_inc(sem["scale_step"], 1)
                dve.wait_ge(sem["gam_ready"], value(b, "gam_ready", p + 1))
                dve.wait_ge(sem["scale_step"], value(b, "scale_step", 4 * p + 3))
                V.tensor_tensor(b2g[:, p], b2[:, 1], gam[:, p, 0, 1], ALU.mult).then_inc(sem["scales_ready"], 1)

            def right_sides(b, p):
                dve.wait_ge(sem["vt_psum"], value(b, "vt_psum", p + 1))
                for c in range(NC):
                    V.tensor_tensor(rv[:, p, c],
                                    bank[6][0:C, c * QH * DH:(c + 1) * QH * DH].rearrange("p (h d) -> p h d", h=QH),
                                    over(brk[:, c], DH, 2), ALU.mult).then_inc(sem["rv_ready"], 1)

            def decayed(b, p, c):
                dve.wait_ge(sem["pairs_psum"], value(b, "pairs_psum", nth(p, c)))
                dve.wait_ge(sem["decays_ready"], value(b, "decays_ready", nth(p, c)))
                if c:
                    dve.wait_ge(sem["l14_ready"], value(b, "l14_ready", nth(p, 0)))
                elif not is_first(b, p):
                    dve.wait_ge(sem["l14_ready"], before(b, p, "l14_ready", 2))
                for h_ in range(QH):
                    V.scalar_tensor_tensor(l_[:, h_, :], bank[5 + h_ // 2][0:C, 0:C], b2[:, c, h_:h_ + 1],
                                           e_[:, c, h_, :], ALU.mult, ALU.mult).then_inc(sem["l_part"], 1)
                for kk in range(2):
                    V.tensor_tensor(p_[:, 2 * kk:2 * kk + 2, :], over(bank[5 + kk][0:C, C:2 * C], 2, 1),
                                    e_[:, c, 2 * kk:2 * kk + 2, :], ALU.mult).then_inc(sem["p_part"], 1)

            def gather_blocks(b, p, c):
                if c == 0 and not is_first(b, p):
                    dve.wait_ge(sem["blocks_out"], before(b, p, "blocks_out", 16))
                dve.wait_ge(sem["l14_ready"], value(b, "l14_ready", nth(p, c)))
                V.tensor_reduce(lc[:, QH * c:QH * (c + 1)], l14[:, c].rearrange("p h (q j) -> p h j q", q=NB),
                                AX.X, ALU.add).then_inc(sem["lc_ready"], 1)

            def read_pt(b, p, c):
                dve.wait_ge(sem["pt_psum"], value(b, "pt_psum", nth(p, c)))
                V.tensor_tensor(pt[:, p, c], quad(bank[5], C), over(upto, QH, 1), ALU.mult
                                ).then_inc(sem["pt_ready"], 1)

            def read_y(b, p, lv, c):
                dve.wait_ge(sem["y_psum"], value(b, "y_psum", 4 * p + 2 * lv + c + 1))
                V.tensor_tensor(y[:, c], quad(bank[2 * c + lv], C), over(mask[:, LEVEL + lv, :], QH, 1), ALU.mult
                                ).then_inc(sem["y_ready"], 1)

            def update_x(b, p, lv, c):
                par = p % 2
                if lv == 0:
                    dve.wait_ge(sem["xn_psum"], value(b, "xn_psum", nth(p, c)))
                    V.tensor_tensor(xn[:, par, c], xn[:, par, c], quad(bank[2 * c + 1], C), ALU.subtract
                                    ).then_inc(sem["xn_ready"], 1)
                else:
                    dve.wait_ge(sem["xt_psum"], value(b, "xt_psum", nth(p, c)))
                    V.tensor_tensor(xt[:, par, c], xt[:, par, c], quad(bank[2 * c], C), ALU.subtract
                                    ).then_inc(sem["xt_ready"], 1)

            def solved(b, p, c):
                dve.wait_ge(sem["u2_psum"], value(b, "u2_psum", nth(p, c)))
                V.tensor_tensor(u[:, c], u1[:, c], quad(bank[2 * c + 1], DH), ALU.subtract).then_inc(sem["u_ready"], 1)

            def to_state(b, p):
                dve.wait_ge(sem["u_ready"], value(b, "u_ready", nth(p, 0)))
                V.tensor_tensor(us[:], u[:, 0], over(gam[:, p, 1, 0], DH, 2), ALU.mult).then_inc(sem["us_ready"], 1)

            def carried(b, p):
                if not is_first(b, p):
                    dve.wait_ge(sem["ogT_psum"], before(b, p, "ogT_psum", 1))
                dve.wait_ge(sem["carry_psum"], value(b, "carry_psum", p + 1))
                for kk in range(2):
                    hs = slice(2 * kk, 2 * kk + 2)
                    src = bank[3 - kk][0:C, 0:4 * DH].rearrange("p (a r d) -> p a r d", a=2, r=2)
                    V.tensor_tensor(tmp[:, hs, :], src[:, 0], over(b2g[:, p, hs], DH, 2), ALU.mult
                                    ).then_inc(sem["carry_part"], 1)
                    V.tensor_tensor(o[:, 1, hs, :], src[:, 1], over(gam[:, p, 0, 1, hs], DH, 2), ALU.mult
                                    ).then_inc(sem["carry_part"], 1)
                dve.wait_ge(sem["carry_part"], value(b, "carry_part", 4 * (p + 1)))
                V.tensor_tensor(rv[:, p, 1], rv[:, p, 1], tmp[:], ALU.subtract).then_inc(sem["r_ready"], 1)

            def output_1(b, p):
                dve.wait_ge(sem["o_psum"], value(b, "o_psum", nth(p, 1)))
                V.tensor_tensor(o[:, 1], o[:, 1], quad(bank[2], DH), ALU.add).then_inc(sem["o1_ready"], 1)

            def mean_squares(b, p):
                dve.wait_ge(sem["osq_ready"], value(b, "osq_ready", p + 1))
                V.tensor_reduce(oss[:, 0], osq[:], AX.X, ALU.add).then_inc(sem["oss_ready"], 1)
                dve.wait_ge(sem["oss_ready"], value(b, "oss_ready", p + 1))
                V.tensor_tensor(oss[:, 1], oss[:, 0], rq2[:, p], ALU.mult).then_inc(sem["oms_ready"], 1)

            def gated(b, p):
                dve.wait_ge(sem["zc_ready"], value(b, "zc_ready", p + 1))
                V.tensor_tensor(o[:], o[:], zc[:], ALU.mult).then_inc(sem["og_ready"], 1)

            def front_alone(b, p):
                convolve(b, p, 0)
                silu(b, p, 0)
                convolve(b, p, 1)
                silu(b, p, 1)
                silu_z(b, p)
                scales(b, p)
                for c in range(NC):
                    decayed(b, p, c)
                    read_pt(b, p, c)
                    gather_blocks(b, p, c)
                right_sides(b, p)

            def prologue():
                V.memset(raw[:, :, 0:TAPS - 1], 0.0)
                V.memset(lc[:, NA:], 0.0)
                for name, tensor in full.items():
                    if name != "mask":
                        V.memset(tensor[:], 0.0)
                V.memset(eps_ln[:], EPS_LN)
                V.memset(eps_head[:], EPS_HEAD)
                V.memset(neg_half[:], -0.5)
                V.memset(ones[:], 1.0)
                V.memset(active[:], 0.0)
                dve.wait_ge(sem["weights"], 16 * len(loads))
                dve.wait_ge(sem["act_setup"], 1)
                V.tensor_tensor(pos_b[:], pos_b[:], over(b_row[:], NC, 1), ALU.add).then_inc(sem["dve_setup"], 1)
                V.tensor_scalar(neg_a[:], neg_a[:], -1.0, None, ALU.mult).then_inc(sem["dve_setup"], 1)
                V.tensor_scalar(w_out[:], w_out[:], norm_w[:], 0.5, ALU.mult, ALU.mult).then_inc(sem["dve_setup"], 1)
                V.tensor_scalar(conv_w[:], conv_w[:], 0.5, None, ALU.mult).then_inc(sem["dve_setup"], 1)
                dve.wait_ge(sem["dve_setup"], 4)
                V.memset(scratch[:, 0:1], 0.0).then_inc(sem["setup"], 1)
                V.memset(scratch[:, 1:2], 0.0).then_inc(sem["h1_stored"], 16)
                V.memset(scratch[:, 2:3], 0.0).then_inc(sem["out_stored"], 16)
                V.memset(scratch[:, 7:8], 0.0).then_inc(sem["r_stored"], 16)
                embedding(0)
                layer_scale(0, h_new, hn, "")
                gate_inputs(0)
                gate_fractions(0)
                gate_series(0, range(len(LOG_TERMS)))
                gate_logs(0)
                move_h(0)
                front_alone(0, 0)
                front_alone(0, 1)

            def slot(b, p, tail, more):
                a, n = front_of(b, p, more), next_of(b, p, more)
                is_tail, is_head = p == 0 and tail, p == 1 and more
                before_ = (b, p - 1) if p else (b - 1, NP - 1) if tail else None
                read_y(b, p, 0, 0)
                if p == 2 and more:
                    gate_series(b + 1, range(4, len(LOG_TERMS)))
                if before_:
                    mean_squares(*before_)
                read_y(b, p, 0, 1)
                if p == 2 and more:
                    gate_logs(b + 1)
                update_x(b, p, 0, 0)
                update_x(b, p, 0, 1)
                if a:
                    convolve(*a, 0, [0])
                read_y(b, p, 1, 0)
                if a:
                    convolve(*a, 0, [1])
                read_y(b, p, 1, 1)
                if a:
                    convolve(*a, 0, [2])
                if before_:
                    gated(*before_)
                update_x(b, p, 1, 0)
                if a:
                    silu(*a, 0)
                update_x(b, p, 1, 1)
                if a:
                    silu_z(*a)
                    convolve(*a, 1)
                if is_head:
                    embedding(b + 1)
                if is_tail:
                    residual(b - 1)
                    layer_stats(b - 1, h1, "2")
                    move_h(b)
                solved(b, p, 0)
                to_state(b, p)
                if a:
                    scales(*a)
                    decayed(*a, 0)
                if is_tail:
                    layer_scale(b - 1, h1, xf, "2")
                if is_head:
                    layer_scale(b + 1, h_new, hn, "")
                carried(b, p)
                if a:
                    read_pt(*a, 0)
                    gather_blocks(*a, 0)
                    silu(*a, 1)
                    decayed(*a, 1)
                if is_head:
                    gate_inputs(b + 1)
                solved(b, p, 1)
                if is_head:
                    gate_fractions(b + 1)
                if is_tail:
                    routing(b - 1)
                if a:
                    read_pt(*a, 1)
                    gather_blocks(*a, 1)
                output_1(b, p)
                if a:
                    right_sides(*a)
                if is_head:
                    gate_series(b + 1, range(4))
                if is_tail:
                    finish(b - 1)

            def epilogue():
                b = NI - 1
                mean_squares(b, NP - 1)
                gated(b, NP - 1)
                residual(b)
                layer_stats(b, h1, "2")
                layer_scale(b, h1, xf, "2")
                routing(b)
                finish(b)

            images(dve, prologue, slot, epilogue)

            dve.wait_ge(sem["prob_step"], value(NI - 1, "prob_step"))
            V.memset(scratch[:, 5:6], 0.0).then_inc(sem["active_summed"], 1)
            dve.wait_ge(sem["count_psum"], 1)
            V.tensor_reduce(scratch[0:1, 6:7], bank[0][0:1, 0:NC], AX.X, ALU.add).then_inc(sem["dve_setup"], 1)
            dve.wait_ge(sem["dve_setup"], 5)
            V.tensor_copy(count[0:1, 0:1], scratch[0:1, 6:7]).then_inc(sem["count_ready"], 1)
            dve.wait_ge(sem["count_ready"], 1)
            with dve.If(dve.value_load(count[0:1, 0:1]) > 0):
                with dve.Fori(0, NI) as b:
                    dve.wait_ge(sem["r_loaded"], value(b, "r_loaded"))
                    layer_stats(b, h1, "3")
                    layer_scale(b, h1, xf, "3")
                    V.tensor_copy(r_prob[:], prob[:, bass.ds(b, 1)].rearrange("p a c e -> p (a c) e")
                                  ).then_inc(sem["r_prob_ready"], 1)
                    dve.wait_ge(sem["r_prob_ready"], value(b, "r_prob_ready"))
                    for e in range(NE):
                        for c in range(NC):
                            dve.wait_ge(sem["r_y_psum"], value(b, "r_y_psum", 2 * e + c + 1))
                            if e:
                                dve.wait_ge(sem["r_added"], value(b, "r_added", 2 * (e - 1) + c + 1))
                            V.scalar_tensor_tensor(out_t[:, c], bank[2 + c][0:C, 0:D], r_prob[:, c, e:e + 1],
                                                   out_t[:, c], ALU.mult, ALU.add).then_inc(sem["r_added"], 1)


def kernel(**inputs):
    import concourse.bacc as bacc
    from concourse.bass_utils import run_bass_kernel_spmd

    def rows(a, k):
        a = np.asarray(a)
        return np.ascontiguousarray(a.reshape(k, 128, a.shape[1]).transpose(1, 0, 2))

    x = np.asarray(inputs["x"])
    n = x.shape[0]
    patches = x.reshape(n, 3, SIDE, 16, SIDE, 16).transpose(0, 1, 3, 5, 2, 4).reshape(n, KP, 128, T)
    order = np.concatenate([np.r_[128 * p:128 * (p + 1), HK * DH + 128 * p:HK * DH + 128 * (p + 1),
                                  2 * HK * DH + 256 * p:2 * HK * DH + 256 * (p + 1)] for p in range(NP)])
    small_c, eye_lane = consts()
    arrays = {
        "x": np.ascontiguousarray(patches.transpose(0, 2, 1, 3)),
        "w_embed": rows(inputs["L0_tok_W_embed"], KP),
        "b_embed": np.asarray(inputs["L0_tok_b_embed"]),
        "pos": np.ascontiguousarray(np.asarray(inputs["L0_tok_pos_embed"]).reshape(NC, C, D).transpose(1, 0, 2)),
        "w_qkv": rows(np.asarray(inputs["L0_attn_W_qkv"])[:, order], KD),
        "w_z": rows(inputs["L0_attn_W_z"], KD),
        "w_ba": rows(np.concatenate([np.asarray(inputs["L0_attn_W_b"]), np.asarray(inputs["L0_attn_W_a"])], 1), KD),
        "dt_bias": np.asarray(inputs["L0_attn_dt_bias"]),
        "a_log": np.asarray(inputs["L0_attn_A_log"]),
        "conv_w": rows(np.asarray(inputs["L0_attn_conv_w"])[order], NP * CT),
        "norm_w": np.ascontiguousarray(np.tile(np.asarray(inputs["L0_attn_norm_w"]), 2)[:, None]),
        "w_out": rows(inputs["L0_attn_W_out"], VT),
        "w_s1": rows(inputs["L0_ffn_Ws1"], KD),
        "w_s2": np.asarray(inputs["L0_ffn_Ws2"]),
        "w_1": np.ascontiguousarray(np.asarray(inputs["L0_ffn_W1"]).reshape(NE, KD, 128, F).transpose(2, 1, 0, 3)
                                    .reshape(128, KD, NE * F)),
        "w_2": np.ascontiguousarray(np.asarray(inputs["L0_ffn_W2"]).transpose(1, 0, 2)),
        "w_r": rows(inputs["L0_ffn_Wr"], KD),
        "masks": masks(), "ident": np.eye(128, dtype=np.float32), "small_c": small_c, "eye_lane": eye_lane,
    }
    nc = bacc.Bacc("TRN2", target_bir_lowering=False, num_devices=1)
    t = {k: nc.dram_tensor(f"in_{k}", a.shape, F32, kind="ExternalInput").ap() for k, a in arrays.items()}
    t["out"] = nc.dram_tensor("out", (n, T, D), F32, kind="ExternalOutput").ap()
    units = NAX * (C - 1) + BK * (NAX - 1) + 1
    t["blocks"] = nc.dram_tensor("blocks", (units, BK), F32, kind="Internal").ap()
    t["inverses"] = nc.dram_tensor("inverses", (units, 2 * BK), F32, kind="Internal").ap()
    t["h1"] = nc.dram_tensor("h1_kept", (n, C, NC, D), F32, kind="Internal").ap()
    build(nc, t, n)
    r = run_bass_kernel_spmd(nc, [{f"in_{k}": a for k, a in arrays.items()}], core_ids=[0])
    return r.results[0]["out"]
```
